# Optimizing a Trainium2 kernel written in Bass

```python
import numpy as np
import jax
import jax.numpy as jnp

def _softmax(x, axis=-1):
    return jax.nn.softmax(x, axis=axis)

def _gelu(x):
    return jax.nn.gelu(x, approximate=True)

def _silu(x):
    return jax.nn.silu(x)

def _sigmoid(x):
    return jax.nn.sigmoid(x)

def _layernorm(x, axis=-1, eps=1e-05):
    m = jnp.mean(x, axis=axis, keepdims=True)
    v = jnp.var(x, axis=axis, keepdims=True)
    return (x - m) / jnp.sqrt(v + eps)

def _scatter_add(tgt, idx, src, axis=0):
    return tgt.at[idx].add(src)

def _segment_sum(src, seg, n):
    return jax.ops.segment_sum(src, seg, n)
kernel_name = 'mk_decoder_postln_d1_seqx_r8_1fca56'

def setup_inputs(seed: int=0):
    np.random.seed(seed)
    _w = jnp.asarray

    def _rec_inputs():
        import jax
        import jax.numpy as jnp
        _rk = jax.random.key(seed)
        x = -0.0003929 + 0.9999 * jax.random.normal(jax.random.fold_in(_rk, 1), (32, 64, 512), jnp.float32)
        _lenS = 64 - jax.random.randint(jax.random.fold_in(_rk, 7), (32,), 0, max(1, 64 // 4) + 1, jnp.int32)
        _lenS2 = 64 - jax.random.randint(jax.random.fold_in(_rk, 8), (32,), 0, max(1, 64 // 4) + 1, jnp.int32)
        _ctx_4096P = jax.random.normal(jax.random.fold_in(_rk, 11), (32, 16, 512), jnp.float32)
        _ctx_4096c = jax.random.dirichlet(jax.random.fold_in(_rk, 511), 0.3 * jnp.ones((16,), jnp.float32), (32, 64))
        _ctx_4096t = jnp.einsum('bsk,bkd->bsd', _ctx_4096c, _ctx_4096P)
        _ctx_4096t = _ctx_4096t * jax.lax.rsqrt(jnp.mean(jnp.square(_ctx_4096t)) + 1e-12) * 0.953939
        ctx_4096 = 2.81802e-05 + 1.00001 * (_ctx_4096t + 0.3 * jax.random.normal(jax.random.fold_in(_rk, 611), (32, 64, 512), jnp.float32))
        return (x, ctx_4096)
    x, ctx_4096 = _rec_inputs()

    def _L0_attn_setup():
        import jax, jax.numpy as jnp
        import numpy as np
        import math
        DIM, NH, NKV, HD = (512, 32, 8, 128)
        BLOCK, NBLK, TOPK = (32, 128, 16)

        def apply_rope(x, cos, sin):
            b, l, h, d = x.shape
            xr = x.reshape(b, l, h, d // 2, 2)
            xe, xo = (xr[..., 0], xr[..., 1])
            c = cos[None, :, None, :]
            s = sin[None, :, None, :]
            oe = xe * c - xo * s
            oo = xe * s + xo * c
            return jnp.stack([oe, oo], axis=-1).reshape(b, l, h, d)
        key = jax.random.key(seed)
        ks = jax.random.split(key, 8)
        x = jax.random.normal(ks[0], (1, 1, DIM), dtype=jnp.float32)
        start_pos = 512
        inv_freq = 1.0 / 500000.0 ** (np.arange(0, HD, 2, dtype=np.float32) / HD)
        ang = np.float32(start_pos) * inv_freq
        freqs_cos = jnp.asarray(np.cos(ang))[None, :]
        freqs_sin = jnp.asarray(np.sin(ang))[None, :]
        sc = 0.02
        wq = jax.random.normal(ks[1], (NH * HD, DIM), dtype=jnp.float32) * sc
        wk = jax.random.normal(ks[2], (NKV * HD, DIM), dtype=jnp.float32) * sc
        wv = jax.random.normal(ks[3], (NKV * HD, DIM), dtype=jnp.float32) * sc
        wo = jax.random.normal(ks[4], (DIM, NH * HD), dtype=jnp.float32) * sc
        k_cache = jax.random.normal(ks[5], (NBLK, BLOCK, NKV, HD), dtype=jnp.float32)
        v_cache = jax.random.normal(ks[6], (NBLK, BLOCK, NKV, HD), dtype=jnp.float32)
        block_idx = jnp.sort(jax.random.randint(ks[7], (TOPK,), 0, NBLK, dtype=jnp.int32))
        return {'x': x, 'freqs_cos': freqs_cos, 'freqs_sin': freqs_sin, 'wq': wq, 'wk': wk, 'wv': wv, 'wo': wo, 'k_cache': k_cache, 'v_cache': v_cache, 'block_idx': block_idx}
    _L0_attn_all = _L0_attn_setup()
    _L0_attn_in = {k: v for k, v in _L0_attn_all.items() if k in ('freqs_cos', 'freqs_sin', 'wq', 'wk', 'wv', 'wo', 'k_cache', 'v_cache', 'block_idx')}
    del _L0_attn_all

    def _L0_xattn_setup():
        import jax, jax.numpy as jnp
        import numpy as np
        HID = 512
        NHEAD = 32
        NKV = 8
        HDIM = 128
        G = NHEAD // NKV
        key = jax.random.key(seed)
        ks = jax.random.split(key, 6)
        s = 0.02
        B, L = (2, 256)
        return {'query': jax.random.normal(ks[0], (B, L, HID), jnp.float32), 'kv': jax.random.normal(ks[1], (B, L, HID), jnp.float32), 'Wq': jax.random.normal(ks[2], (HID, NHEAD * HDIM), jnp.float32) * s, 'bq': jnp.zeros((NHEAD * HDIM,), jnp.float32), 'Wkv': jax.random.normal(ks[3], (HID, 2 * NKV * HDIM), jnp.float32) * s, 'bkv': jnp.zeros((2 * NKV * HDIM,), jnp.float32), 'Wo': jax.random.normal(ks[4], (NHEAD * HDIM, HID), jnp.float32) * s, 'bo': jnp.zeros((HID,), jnp.float32)}
    _L0_xattn_all = _L0_xattn_setup()
    _L0_xattn_in = {k: v for k, v in _L0_xattn_all.items() if k in ('Wq', 'bq', 'Wkv', 'bkv', 'Wo', 'bo')}
    del _L0_xattn_all

    def _L0_ffn_setup():
        import jax, jax.numpy as jnp
        import numpy as np
        C_CLAMP = 0.5
        EPS = 1e-06
        key = jax.random.key(seed)
        ks = jax.random.split(key, 6)
        B_, S, D, O, R, E = (4, 256, 512, 512, 16, 8)
        x = jax.random.normal(ks[0], (B_, S, D), dtype=jnp.float32)
        W = jax.random.normal(ks[1], (O, D), dtype=jnp.float32) * (1.0 / np.sqrt(D))
        b = jax.random.normal(ks[2], (O,), dtype=jnp.float32) * 0.01
        A = jax.random.normal(ks[3], (E, D, R), dtype=jnp.float32) * (1.0 / np.sqrt(D))
        Bm = jax.random.normal(ks[4], (E, R, O), dtype=jnp.float32) * (1.0 / np.sqrt(R))
        p_scores = jax.random.uniform(ks[5], (E,), dtype=jnp.float32)
        return {'x': x, 'W': W, 'b': b, 'A': A, 'B': Bm, 'p_scores': p_scores}
    _L0_ffn_all = _L0_ffn_setup()
    _L0_ffn_in = {k: v for k, v in _L0_ffn_all.items() if k in ('W', 'b', 'A', 'B', 'p_scores')}
    del _L0_ffn_all
    return {'x': x, 'ctx_4096': ctx_4096, 'L0_attn_freqs_cos': _L0_attn_in['freqs_cos'], 'L0_attn_freqs_sin': _L0_attn_in['freqs_sin'], 'L0_attn_wq': _L0_attn_in['wq'], 'L0_attn_wk': _L0_attn_in['wk'], 'L0_attn_wv': _L0_attn_in['wv'], 'L0_attn_wo': _L0_attn_in['wo'], 'L0_attn_k_cache': _L0_attn_in['k_cache'], 'L0_attn_v_cache': _L0_attn_in['v_cache'], 'L0_attn_block_idx': _L0_attn_in['block_idx'], 'L0_xattn_Wq': _L0_xattn_in['Wq'], 'L0_xattn_bq': _L0_xattn_in['bq'], 'L0_xattn_Wkv': _L0_xattn_in['Wkv'], 'L0_xattn_bkv': _L0_xattn_in['bkv'], 'L0_xattn_Wo': _L0_xattn_in['Wo'], 'L0_xattn_bo': _L0_xattn_in['bo'], 'L0_ffn_W': _L0_ffn_in['W'], 'L0_ffn_b': _L0_ffn_in['b'], 'L0_ffn_A': _L0_ffn_in['A'], 'L0_ffn_B': _L0_ffn_in['B'], 'L0_ffn_p_scores': _L0_ffn_in['p_scores']}

def reference(x, ctx_4096, L0_attn_freqs_cos, L0_attn_freqs_sin, L0_attn_wq, L0_attn_wk, L0_attn_wv, L0_attn_wo, L0_attn_k_cache, L0_attn_v_cache, L0_attn_block_idx, L0_xattn_Wq, L0_xattn_bq, L0_xattn_Wkv, L0_xattn_bkv, L0_xattn_Wo, L0_xattn_bo, L0_ffn_W, L0_ffn_b, L0_ffn_A, L0_ffn_B, L0_ffn_p_scores):
    import jax
    import jax.numpy as jnp

    def _L0_attn_ref(x, freqs_cos, freqs_sin, wq, wk, wv, wo, k_cache, v_cache, block_idx):
        import jax, jax.numpy as jnp
        import numpy as np
        import math
        DIM, NH, NKV, HD = (512, 32, 8, 128)
        BLOCK, NBLK, TOPK = (32, 128, 16)

        def apply_rope(x, cos, sin):
            b, l, h, d = x.shape
            xr = x.reshape(b, l, h, d // 2, 2)
            xe, xo = (xr[..., 0], xr[..., 1])
            c = cos[None, :, None, :]
            s = sin[None, :, None, :]
            oe = xe * c - xo * s
            oo = xe * s + xo * c
            return jnp.stack([oe, oo], axis=-1).reshape(b, l, h, d)
        b, l, _ = x.shape
        n_rep = NH // NKV
        q = (x @ wq.T).reshape(b, l, NH, HD)
        k = (x @ wk.T).reshape(b, l, NKV, HD)
        v = (x @ wv.T).reshape(b, l, NKV, HD)
        q = apply_rope(q, freqs_cos, freqs_sin)
        k = apply_rope(k, freqs_cos, freqs_sin)
        k_sel = k_cache[block_idx].reshape(-1, NKV, HD)
        v_sel = v_cache[block_idx].reshape(-1, NKV, HD)
        k_full = jnp.concatenate([k_sel, k[0]], axis=0)
        v_full = jnp.concatenate([v_sel, v[0]], axis=0)
        k_full = jnp.repeat(k_full.transpose(1, 0, 2)[None], n_rep, axis=1)
        v_full = jnp.repeat(v_full.transpose(1, 0, 2)[None], n_rep, axis=1)
        qh = q.transpose(0, 2, 1, 3)
        scores = jnp.einsum('bhld,bhtd->bhlt', qh, k_full) / math.sqrt(HD)
        attn = jax.nn.softmax(scores, axis=-1)
        out = jnp.einsum('bhlt,bhtd->bhld', attn, v_full)
        out = out.transpose(0, 2, 1, 3).reshape(b, l, NH * HD)
        return out @ wo.T

    def _L0_xattn_ref(query, kv, Wq, bq, Wkv, bkv, Wo, bo):
        import jax, jax.numpy as jnp
        import numpy as np
        HID = 512
        NHEAD = 32
        NKV = 8
        HDIM = 128
        G = NHEAD // NKV
        B, L, _ = query.shape
        Lk = kv.shape[1]
        scale = jnp.asarray(1.0 / np.sqrt(HDIM), query.dtype)
        q = (query @ Wq + bq).reshape(B, L, NKV, G, HDIM)
        k_, v_ = jnp.split(kv @ Wkv + bkv, 2, axis=-1)
        k = k_.reshape(B, Lk, NKV, HDIM)
        v = v_.reshape(B, Lk, NKV, HDIM)
        scores = jnp.einsum('blkgd,bmkd->bkglm', q, k) * scale
        attn = jax.nn.softmax(scores, axis=-1)
        o = jnp.einsum('bkglm,bmkd->blkgd', attn, v).reshape(B, L, NHEAD * HDIM)
        return o @ Wo + bo

    def _L0_ffn_ref(x, W, b, A, B, p_scores):
        import jax, jax.numpy as jnp
        import numpy as np
        C_CLAMP = 0.5
        EPS = 1e-06
        z = jnp.einsum('bsd,od->bso', x, W) + b
        u = jnp.einsum('bsd,edr->ebsr', x, A)
        m = jnp.einsum('ebsr,ero,e->bso', u, B, p_scores)
        norm_z = jnp.linalg.norm(z, axis=-1, keepdims=True)
        norm_m = jnp.linalg.norm(m, axis=-1, keepdims=True)
        gamma = jnp.minimum(C_CLAMP * norm_z / (norm_m + EPS), 1.0)
        return z + gamma * m
    x = _layernorm(x + _L0_attn_ref(x, L0_attn_freqs_cos, L0_attn_freqs_sin, L0_attn_wq, L0_attn_wk, L0_attn_wv, L0_attn_wo, L0_attn_k_cache, L0_attn_v_cache, L0_attn_block_idx), axis=-1)
    x = _layernorm(x + _L0_xattn_ref(x, ctx_4096, L0_xattn_Wq, L0_xattn_bq, L0_xattn_Wkv, L0_xattn_bkv, L0_xattn_Wo, L0_xattn_bo), axis=-1)
    x = _layernorm(x + _L0_ffn_ref(x, L0_ffn_W, L0_ffn_b, L0_ffn_A, L0_ffn_B, L0_ffn_p_scores), axis=-1)
    return x

_drawn_inputs = setup_inputs


def setup_inputs(seed=0):
    import zlib

    import numpy as np

    out = dict(_drawn_inputs(seed))
    spreads = {'L0_xattn_bq': (0.0, 0.8), 'L0_xattn_bkv': (0.0, 0.1), 'L0_xattn_bo': (0.0, 0.1)}
    factors = {'L0_attn_freqs_sin': 3.747,
     'L0_attn_wk': 8.0,
     'L0_attn_wv': 7.068,
     'L0_ffn_b': 8.0,
     'L0_attn_k_cache': 8.0,
     'L0_attn_v_cache': 8.0}
    for name, (base, spread) in spreads.items():
        noise = np.random.default_rng([zlib.crc32(name.encode()), seed]).standard_normal(out[name].shape)
        drawn = base * np.exp(spread * noise) if base else spread * noise
        out[name] = jnp.asarray(drawn.astype(out[name].dtype))
    for name, factor in factors.items():
        out[name] = (out[name] * factor).astype(out[name].dtype)
    return out
```

```python
import concourse.bass as bass
from concourse import mybir
from contextlib import ExitStack

F32 = mybir.dt.float32
F32R = mybir.dt.float32r
I32 = mybir.dt.int32
U32 = mybir.dt.uint32
ALU = mybir.AluOpType
ACT = mybir.ActivationFunctionType
AX = mybir.AxisListType

D = 512
T = 2048
NT = T // 128
NC = D // 128
NH = 32
G = 8
HD = 128
KEYS = 576
HALF = KEYS // 2
SCALE = float(HD) ** -0.5
LN_EPS = 1e-5
E_R = 128


class Count:

    def __init__(self, h):
        self.h, self.n = h, 0


class Queue:

    def __init__(self):
        self.ops, self.seen = [], {}

    def wait(self, *tokens):
        for t in tokens:
            if t is None:
                continue
            if isinstance(t, list):
                self.wait(*t)
                continue
            c, v = t
            if self.seen.get(id(c), 0) < v:
                self.seen[id(c)] = v
                self.ops.append(lambda e, h=c.h, v=v: e.wait_ge(h, v))

    def do(self, fn, count=None, by=1):
        if count is None:
            self.ops.append(fn)
            return None
        self.ops.append(lambda e: fn(e).then_inc(count.h, by))
        count.n += by
        return (count, count.n)

    def run(self, e):
        for op in self.ops:
            op(e)


def decoder_kernel(nc, x, ctx_in, fcos, fsin, wq, wk, wv, wo, k_cache, v_cache, block_idx,
                   xWq, xbq, xWkv, xbkv, xWo, xbo, fW, fb, fA, fB, fp, out):
    with ExitStack() as top:
        pe, dve, act, pool, sp = Queue(), Queue(), Queue(), Queue(), Queue()

        def sem(name):
            return Count(top.enter_context(nc.semaphore(name)))

        def sb(name, shape, dt=F32, scope=top):
            return scope.enter_context(nc.sbuf_tensor(name, shape, dt))

        def pair(name, shape, scope=top):
            return sb(name + "h", shape, F32R, scope), sb(name + "l", shape, F32R, scope)

        def f(ap):
            return ap.bitcast(F32)

        xf = x.rearrange("a b d -> (a b) d")
        cf = ctx_in.rearrange("a b d -> (a b) d")
        of = out.rearrange("a b d -> (a b) d")

        bank = [top.enter_context(nc.psum_tensor(f"bank{i}", [128, 512], F32)) for i in range(2)]
        big = [top.enter_context(nc.psum_tensor(f"big{i}", [128, 2, 512], F32)) for i in range(3)]
        ps_pt = [bank[0], bank[1]]
        ps_s = [big[0], big[1]]
        ps_o = big[2][:, 0, :]
        ps_m = big[2][:, 1, :]

        c_init = sem("c_init")
        c_x = [sem(f"c_x{i}") for i in range(4)]
        c_cst = sem("c_cst")
        c_xtr = sem("c_xtr")
        c_xhi = sem("c_xhi")
        c_xlo = sem("c_xlo")
        c_raw = [sem(f"c_raw{i}") for i in range(4)]
        c_gk = sem("c_gk")
        c_gv = sem("c_gv")
        c_wtr = sem("c_wtr")
        c_whi = sem("c_whi")
        c_wlo = sem("c_wlo")
        c_kv = sem("c_kv")
        c_kvd = sem("c_kvd")
        c_kva = sem("c_kva")
        c_kvp = sem("c_kvp")
        c_vn = sem("c_vn")
        c_ctx = [sem(f"c_ctx{i}") for i in range(2)]
        c_q = sem("c_q")
        c_qhi = sem("c_qhi")
        c_qlo = sem("c_qlo")
        c_s = sem("c_s")
        c_max = sem("c_max")
        c_exp = sem("c_exp")
        c_rec = sem("c_rec")
        c_p = sem("c_p")
        c_tr = sem("c_tr")
        c_phi = sem("c_phi")
        c_plo = sem("c_plo")
        c_pv = sem("c_pv")
        c_ohi = sem("c_ohi")
        c_olo = sem("c_olo")
        c_wo = sem("c_wo")
        c_add = sem("c_add")
        c_ln = sem("c_ln")
        c_lna = sem("c_lna")
        c_bo = sem("c_bo")
        c_sub = sem("c_sub")
        c_sum = sem("c_sum")
        c_ff = sem("c_ff")
        c_ffa = sem("c_ffa")
        c_ffd = sem("c_ffd")
        c_out = sem("c_out")

        ident = sb("ident", [128, 128])
        xacc = sb("xacc", [128, NT, D])
        stat = sb("stat", [128, NT, 6])
        mv = sb("mv", [128, NT, 2])
        rstd = sb("rstd", [128, NT])
        bqk = sb("bqk", [128, 48])
        pcol = sb("pcol", [128, 1])

        t_id0 = pool.do(lambda e: e.memset(ident[:, :], 0.0), c_init)
        pool.wait(t_id0)
        t_id = pool.do(lambda e: e.affine_select(
            out=ident[:, :], in_=ident[:, :], compare_op=ALU.not_equal, fill=1.0, base=0,
            pattern=[[-1, 128]], channel_multiplier=1), c_init)

        t_x = []
        for q in range(4):
            t_x.append(sp.do(lambda e, q=q: e.dma_start(
                xacc[:, 4 * q:4 * q + 4, :],
                xf[512 * q:512 * q + 512, :].rearrange("(t p) d -> p t d", p=128)), c_x[q], 16))

        def products(dst, terms, count, first=True, final=True):
            tok = None
            for i, (a, b) in enumerate(terms):
                end = i == len(terms) - 1
                tok = pe.do(lambda e, a=a, b=b, s=first and i == 0, z=final and end:
                            e.matmul(dst, a, b, start=s, stop=z), count if end else None)
            return tok

        def split3(ah, al, bh, bl):
            return [(ah, bh), (ah, bl), (al, bh)]

        def transposes(dst, srcs, count):
            tok = None
            for i, s in enumerate(srcs):
                tok = pe.do(lambda e, i=i, s=s: e.transpose(dst[:, 128 * i:128 * i + 128], s, ident[:, :]),
                            count if i == len(srcs) - 1 else None)
            return tok

        def hi_lo(src, hi, lo, t_src, t_free, c_hi, c_lo):
            act.wait(t_src, t_free)
            a = act.do(lambda e: e.activation(hi, src, ACT.Copy), c_hi)
            dve.wait(a)
            return dve.do(lambda e: e.tensor_tensor(lo, src, f(hi), ALU.subtract), c_lo)

        turn = {}

        def transposed_tile(tt, srcs, t_srcs, hT, lT, col, banks):
            k = turn.setdefault("x", 0)
            turn["x"] += 1
            dst = banks[k % len(banks)]
            pe.wait(t_srcs, t_id, turn.get(("x", k % len(banks))))
            t = transposes(dst, srcs, c_xtr)
            v = dst.rearrange("p (c t) -> p c t", c=NC)
            lo = hi_lo(v, hT[:, :, col:col + 128], lT[:, :, col:col + 128], t, None, c_xhi, c_xlo)
            turn[("x", k % len(banks))] = lo
            return t, lo

        def layernorm(tiles, t_in):
            a, b = tiles[0], tiles[-1] + 1
            dve.wait(t_in)
            for tt in tiles:
                t = dve.do(lambda e, tt=tt: e.bn_stats(stat[:, tt, :], xacc[:, tt, :]), c_ln)
            dve.wait(t)
            for tt in tiles:
                t = dve.do(lambda e, tt=tt: e.bn_aggr(mv[:, tt, :], stat[:, tt, :]), c_ln)
            dve.wait(t)
            t = dve.do(lambda e: e.tensor_scalar(mv[:, a:b, 1], mv[:, a:b, 1], LN_EPS, None, ALU.add), c_ln)
            act.wait(t)
            t = act.do(lambda e: e.activation(rstd[:, a:b], mv[:, a:b, 1], ACT.Sqrt), c_lna)
            dve.wait(t)
            t = dve.do(lambda e: e.reciprocal(rstd[:, a:b], rstd[:, a:b]), c_ln)
            dve.wait(t)
            for tt in tiles:
                t = dve.do(lambda e, tt=tt: e.tensor_scalar(
                    xacc[:, tt, :], xacc[:, tt, :], mv[:, tt, 0:1], rstd[:, tt:tt + 1],
                    ALU.subtract, ALU.mult), c_ln)
            return t

        one = ExitStack()
        xTh, xTl = pair("xT", [128, NC, T], one)
        wqh, wql = pair("wqT", [128, 4, NC, 128], one)
        woh, wol = pair("woT", [128, 3, D], one)
        wkvh, wkvl = pair("wkvT", [128, NC, 128], one)
        raw = sb("raw", [128, 3, 512], F32, one)
        rkv = sb("rkv", [128, 4, 128], F32, one)
        krot = sb("krot", [128, 4, 128], F32, one)
        kTh, kTl = pair("kT", [128, 2, KEYS], one)
        vh, vl = pair("v", [128, 2, 4, 128], one)
        v4a, v4b = sb("v4a", [128, 2, 128], F32R, one), sb("v4b", [128, 2, 128], F32R, one)
        vtmp = sb("vtmp", [64, 128], F32R, one)
        P = sb("P", [128, 8, KEYS + 64], F32, one)
        pth, ptl = pair("pt", [128, 2, 512], one)
        qTh, qTl = pair("qT", [128, 2, 512], one)
        oh, ol = pair("oT", [128, 3, 512], one)
        cosb = sb("cosb", [128, 64], F32, one)
        sinb = sb("sinb", [128, 64], F32, one)
        ccol = sb("ccol", [128, 2], F32, one)
        cs2 = sb("cs2", [128, 1], F32, one)
        bidx = sb("bidx", [128, 4], I32, one)
        prow = sb("prow", [128, 1], I32, one)
        prowf = sb("prowf", [128, 1], F32, one)
        idx0 = sb("idx0", [128, 4], F32, one)
        idx = sb("idx", [128, G, 4], I32, one)
        nmx = sb("nmx", [128, 8], F32, one)
        rsum = sb("rsum", [128, 8], F32, one)
        rrec = sb("rrec", [128, 8], F32, one)

        bi = block_idx.rearrange("(k a) -> a k", a=4)
        for a in range(4):
            t_c = sp.do(lambda e, a=a: e.dma_start(
                bidx[32 * a:32 * a + 32, :], bi[a:a + 1, :].to_broadcast([32, 4]), allow_slow_non_contiguous=True), c_cst, 16)
        sp.do(lambda e: e.dma_start(cosb[:, :], fcos.to_broadcast([128, 64])), c_cst, 16)
        sp.do(lambda e: e.dma_start(sinb[:, :], fsin.to_broadcast([128, 64])), c_cst, 16)
        for i, v in enumerate((fcos, fsin)):
            t_c = sp.do(lambda e, i=i, v=v: e.dma_start(
                ccol[:, i:i + 1], v.rearrange("a (d o) -> (a d) o", o=1).unsqueeze(1).to_broadcast([64, 2, 1]),
                allow_slow_non_contiguous=True),
                c_cst, 16)
        t_row = t_id
        for a in range(4):
            pool.wait(t_row)
            t_row = pool.do(lambda e, a=a: e.iota(prow[32 * a:32 * a + 32, :], [[0, 1]], base=0,
                                                  channel_multiplier=8), c_init)
        dve.wait(t_c, t_row)
        t = dve.do(lambda e: e.tensor_copy(prowf[:, :], prow[:, :]), c_kvd)
        dve.wait(t)
        t = dve.do(lambda e: e.tensor_scalar(idx0[:, :], bidx[:, :], 256.0, prowf[:, 0:1], ALU.mult, ALU.add), c_kvd)
        dve.wait(t)
        for g in range(G):
            t_idx = dve.do(lambda e, g=g: e.tensor_scalar(idx[:, g, :], idx0[:, :], float(g), None, ALU.add), c_kvd)
        t = dve.do(lambda e: e.tensor_scalar(cosb[:, :], cosb[:, :], SCALE, None, ALU.mult), c_kvd)
        t = dve.do(lambda e: e.tensor_scalar(sinb[:, :], sinb[:, :], SCALE, None, ALU.mult), c_kvd)
        t = dve.do(lambda e: e.tensor_tensor(ccol[:, :], ccol[:, :], ccol[:, :], ALU.mult), c_kvd)
        dve.wait(t)
        t = dve.do(lambda e: e.tensor_tensor(cs2[:, :], ccol[:, 0:1], ccol[:, 1:2], ALU.add), c_kvd)
        dve.wait(t)
        t_rot = dve.do(lambda e: e.tensor_scalar(cs2[:, :], cs2[:, :], SCALE, None, ALU.mult), c_kvd)
        t_v4 = t_row
        for b in range(2):
            pool.wait(t_v4)
            t_v4 = pool.do(lambda e, b=b: e.memset(f(v4b[64:128, b, :]), 0.0), c_init)

        kc_v = k_cache.rearrange("n b h d -> (n b h) d")
        vc_v = v_cache.rearrange("n b h d -> (n b h) d")
        wq_v = wq.rearrange("(h p) d -> h p d", p=128)
        wk_v = wk.rearrange("(h p) d -> h p d", p=128)
        wv_v = wv.rearrange("(h p) d -> h p d", p=128)
        wo_v = wo.rearrange("(o p) (h d) -> h p o d", p=128, d=128)

        raw_free = [None] * 3
        raw_n = [0]

        def load_raw(dst_view, src):
            s = raw_n[0] % 3
            raw_n[0] += 1
            sp.wait(raw_free[s])
            return s, sp.do(lambda e: e.dma_start(dst_view(raw[:, s, :]), src), c_raw[s], 16)

        def as_rows(r):
            return r

        def as_blocks(r):
            return r.rearrange("p (o d) -> p o d", d=128)

        m_free = [None]

        def weight(loaded, hi, lo, t_free):
            s, t_in = loaded
            pe.wait(t_in, t_id, m_free[0])
            t = transposes(ps_m, [raw[:, s, 128 * c:128 * c + 128] for c in range(4)], c_wtr)
            raw_free[s] = t
            lo_t = hi_lo(ps_m, hi, lo, t, t_free, c_whi, c_wlo)
            m_free[0] = lo_t
            return lo_t

        t_wq, t_wo, t_kT, t_v = {}, {}, {}, {}
        wq_done, wo_done = {}, {}
        k_done, v_done = {}, {}
        t_xT = [None] * 4
        state = {}

        def flat(ap):
            return ap.rearrange("p c d -> p (c d)")

        def gather(g, what, dst, src, count, t_free):
            pool.wait(t_idx, t_free)
            for b in range(4):
                t = pool.do(lambda e, b=b: e.indirect_dma_start(
                    dst[:, b, :], None, src, bass.IndirectOffsetOnAxis(ap=idx[:, g, b:b + 1].bitcast(U32), axis=0)),
                    count, 16)
            state[what] = t

        def task(kind, n):
            if kind == "wq":
                return ("wq", n, lambda: load_raw(as_rows, wq_v[n]))
            if kind == "wo":
                return ("wo", n, lambda: load_raw(as_blocks, wo_v[n]))
            if kind == "wk":
                return ("wk", n, lambda: load_raw(as_rows, wk_v[n]))
            if kind == "wv":
                return ("wv", n, lambda: load_raw(as_rows, wv_v[n]))
            return (kind, n, lambda: None)

        def run_task(kind, n, loaded):
            if kind == "wq":
                t_wq[n] = weight(loaded, flat(wqh[:, n % 4]), flat(wql[:, n % 4]), wq_done.get(n - 4))
            elif kind == "wo":
                t_wo[n] = weight(loaded, woh[:, n % 3], wol[:, n % 3], wo_done.get(n - 3))
            elif kind in ("wk", "wv"):
                state[kind] = weight(loaded, flat(wkvh[:, :, :]), flat(wkvl[:, :, :]), state.get("wkv_done"))
            elif kind == "gk":
                gather(n, "gk", rkv, kc_v, c_gk, state.get("rkv_done"))
            elif kind == "gv":
                gather(n, "gv", rkv, vc_v, c_gv, state.get("rkv_done"))
            elif kind == "rot":
                b = n % 2
                dve.wait(state["gk"], t_rot, state.get("krot_done"))
                src = rkv[:, :, :].rearrange("p b (d o) -> p b d o", o=2)
                dst = krot[:, :, :].rearrange("p b (d o) -> p b d o", o=2)
                cb = cosb[:, :].unsqueeze(1).to_broadcast([128, 4, 64])
                sn = sinb[:, :].unsqueeze(1).to_broadcast([128, 4, 64])
                for o in range(2):
                    t = dve.do(lambda e, o=o: e.tensor_tensor(dst[:, :, :, o], src[:, :, :, o], cb, ALU.mult), c_kvd)
                dve.wait(t)
                for o in range(2):
                    t = dve.do(lambda e, o=o: e.tensor_tensor(src[:, :, :, o], src[:, :, :, o], sn, ALU.mult), c_kvd)
                dve.wait(t)
                dve.do(lambda e: e.tensor_tensor(dst[:, :, :, 0], dst[:, :, :, 0], src[:, :, :, 1], ALU.add), c_kvd)
                t = dve.do(lambda e: e.tensor_tensor(dst[:, :, :, 1], dst[:, :, :, 1], src[:, :, :, 0], ALU.subtract),
                           c_kvd)
                state["rot"] = t
                state["rkv_done"] = t
            elif kind == "kT":
                b = n % 2
                pe.wait(state["rot"], t_id, m_free[0])
                t = transposes(ps_m, [krot[:, j, :] for j in range(4)], c_kv)
                state["krot_done"] = t
                t_kT[n] = m_free[0] = hi_lo(ps_m, kTh[:, b, 0:512], kTl[:, b, 0:512], t, k_done.get(n - 2),
                                            c_kva, c_kvd)
            elif kind == "kn":
                b = n % 2
                pe.wait(state["wk"], m_free[0], t_xT[0])
                terms = []
                for c in range(NC):
                    terms += split3(wkvh[:, c, :], wkvl[:, c, :], xTh[:, c, 0:64], xTl[:, c, 0:64])
                t = products(ps_m[:, 0:64], terms, c_kv)
                state["wkv_done"] = t
                act.wait(t, t_rot, k_done.get(n - 2))
                hi, lo = kTh[:, b, 512:576], kTl[:, b, 512:576]
                a = act.do(lambda e: e.activation(hi, ps_m[:, 0:64], ACT.Identity, scale=cs2[:, 0:1]), c_kva)
                dve.wait(a)
                m_free[0] = dve.do(lambda e: e.scalar_tensor_tensor(
                    lo, ps_m[:, 0:64], cs2[:, 0:1], f(hi), ALU.mult, ALU.subtract), c_kvd)
                state["kn"] = m_free[0]
            elif kind == "vn":
                b = n % 2
                pe.wait(state["wv"], m_free[0], t_xT[0])
                terms = []
                for c in range(NC):
                    terms += split3(xTh[:, c, 0:64], xTl[:, c, 0:64], wkvh[:, c, :], wkvl[:, c, :])
                t = products(ps_m[0:64, 0:128], terms, c_kv)
                state["wkv_done"] = t
                act.wait(t, v_done.get(n - 2), t_v4)
                act.do(lambda e: e.activation(v4a[0:64, b, :], ps_m[0:64, 0:128], ACT.Copy))
                a = act.do(lambda e: e.activation(v4b[0:64, b, :], ps_m[0:64, 0:128], ACT.Copy), c_kva)
                dve.wait(a, state.get("vn"))
                m_free[0] = d = dve.do(lambda e: e.tensor_tensor(
                    vtmp[:, :], ps_m[0:64, 0:128], f(v4b[0:64, b, :]), ALU.subtract), c_kvd)
                sp.wait(d, v_done.get(n - 2))
                state["vn"] = sp.do(lambda e: e.dma_start(f(v4a[64:128, b, :]), f(vtmp[:, :])), c_vn, 16)
            elif kind == "vs":
                b = n % 2
                act.wait(state["gv"], v_done.get(n - 2))
                a = act.do(lambda e: e.activation(vh[:, b], rkv[:, :, :], ACT.Copy), c_kva)
                pool.wait(a)
                t = pool.do(lambda e: e.tensor_tensor(vl[:, b], rkv[:, :, :], f(vh[:, b]), ALU.subtract), c_kvp)
                state["rkv_done"] = t
                t_v[n] = [t]


        run_task("gk", 0, None)
        banks = [bank[0][:, :], bank[1][:, :], ps_o, big[0][:, 0, :], big[0][:, 1, :], big[1][:, 0, :]]
        pre = [task(*a) for a in (("wk", 0), ("wq", 0), ("wq", 1))]
        loads = [p[2]() for p in pre]
        for q in range(4):
            for tt in range(4 * q, 4 * q + 4):
                _, t_xT[q] = transposed_tile(tt, [xacc[:, tt, 128 * c:128 * c + 128] for c in range(NC)],
                                             t_x[q], xTh, xTl, 128 * tt, banks)
        t_pro = t_xT[3]
        run_task("wk", 0, loads[0])
        run_task("rot", 0, None)
        run_task("kn", 0, None)
        run_task("kT", 0, None)
        run_task("wq", 0, loads[1])
        run_task("wq", 1, loads[2])
        run_task("gv", 0, None)
        run_task("wv", 0, task("wv", 0)[2]())
        run_task("vn", 0, None)
        run_task("vs", 0, None)

        plan = {}
        for g in range(G):
            s = 16 * g
            plan[s] = [("wo", 4 * g)]
            plan[s + 1] = [("wo", 4 * g + 1)]
            plan[s + 2] = [("wq", 4 * g + 2)]
            plan[s + 3] = [("wq", 4 * g + 3)]
            plan[s + 8] = [("wo", 4 * g + 2)]
            plan[s + 9] = [("wo", 4 * g + 3)]
            if g + 1 < G:
                plan[s + 4] = [("gk", g + 1), ("wk", g + 1)]
                plan[s + 5] = [("rot", g + 1), ("kn", g + 1), ("gv", g + 1)]
                plan[s + 6] = [("kT", g + 1)]
                plan[s + 7] = [("vs", g + 1)]
                plan[s + 10] = [("wv", g + 1)]
                plan[s + 11] = [("vn", g + 1)]
                plan[s + 12] = [("wq", 4 * g + 4)]
                plan[s + 13] = [("wq", 4 * g + 5)]
        order = [(s, a) for s in sorted(plan) for a in plan[s]]
        queue = [(s, task(*a)) for s, a in order]
        pending = {}
        nxt = [0]

        def prefetch(upto):
            while nxt[0] < len(queue) and queue[nxt[0]][0] <= upto:
                s, (kind, n, load) = queue[nxt[0]]
                pending[(kind, n)] = load()
                nxt[0] += 1

        UNITS = 128
        t_q, t_s, t_max, t_exp, t_rec, t_p = {}, {}, {}, {}, {}, {}
        t_tr, t_plo, t_pv, t_olo, t_wod = {}, {}, {}, {}, {}
        t_addx = [t_pro] * NT

        def head(u):
            return 2 * (u // 8) + u % 2

        def qg(u):
            return (u % 8) // 2

        def q_pe(u):
            h, c0 = head(u), 512 * qg(u)
            pe.wait(t_wq[h], t_xT[qg(u)], m_free[0])
            terms = []
            for c in range(NC):
                terms += split3(wqh[:, h % 4, c, :], wql[:, h % 4, c, :],
                                xTh[:, c, c0:c0 + 512], xTl[:, c, c0:c0 + 512])
            t = products(ps_m, terms, c_q)
            wq_done[h] = t
            t_q[u] = hi_lo(ps_m, qTh[:, u % 2], qTl[:, u % 2], t, t_s.get(4 * (u - 2) + 3), c_qhi, c_qlo)
            m_free[0] = t_q[u]

        def s_pe(u, t):
            i, b = 4 * u + t, (head(u) // 4) % 2
            pe.wait(t_q[u], t_kT[head(u) // 4], state.get("kn"), t_exp.get(i - 2))
            a, z = 128 * t, 128 * t + 128
            dst = ps_s[i % 2]
            terms = split3(qTh[:, u % 2, a:z], qTl[:, u % 2, a:z], kTh[:, b], kTl[:, b])
            for n, (l, r) in enumerate(terms):
                for k in range(2):
                    last = n == 2 and k == 1
                    tok = pe.do(lambda e, l=l, r=r, k=k, n=n: e.matmul(
                        dst[:, k, 0:HALF], l, r[:, HALF * k:HALF * k + HALF], start=n == 0, stop=n == 2),
                        c_s if last else None)
            t_s[i] = tok
            k_done[head(u) // 4] = tok

        def s_max(u, t):
            i = 4 * u + t
            dve.wait(t_s[i])
            t_max[i] = dve.do(lambda e: e.tensor_reduce(
                nmx[:, i % 8:i % 8 + 1], ps_s[i % 2][:, :, 0:HALF], AX.XY, ALU.max, negate=True), c_max)

        def s_exp(u, t):
            i = 4 * u + t
            act.wait(t_max[i], t_tr.get(5 * (u - 2) + 4))
            t_exp[i] = act.do(lambda e: e.activation(
                P[:, i % 8, 0:KEYS].rearrange("p (k n) -> p k n", k=2), ps_s[i % 2][:, :, 0:HALF], ACT.Exp,
                bias=nmx[:, i % 8:i % 8 + 1], scale=1.0, accum_out=rsum[:, i % 8:i % 8 + 1]), c_exp)

        def s_norm(u, t):
            i = 4 * u + t
            dve.wait(t_exp[i])
            t_rec[i] = dve.do(lambda e: e.reciprocal(rrec[:, i % 8:i % 8 + 1], rsum[:, i % 8:i % 8 + 1]), c_rec)
            pool.wait(t_rec[i])
            d = pool.do(lambda e: e.tensor_scalar(
                P[:, i % 8, KEYS:KEYS + 64], P[:, i % 8, 512:KEYS], rrec[:, i % 8:i % 8 + 1], 1.0,
                ALU.mult, ALU.mult), c_p)
            pool.wait(d)
            t_p[i] = pool.do(lambda e: e.tensor_scalar(
                P[:, i % 8, 0:KEYS], P[:, i % 8, 0:KEYS], rrec[:, i % 8:i % 8 + 1], 1.0, ALU.mult, ALU.mult), c_p)

        def tr_pe(u, j):
            k = 5 * u + j
            pe.wait(t_p[4 * u + 3], t_plo.get(k - 2))
            srcs = []
            for t in range(4):
                r = P[:, (4 * u + t) % 8, :]
                srcs.append(r[:, 128 * j:128 * j + 128])
            t_tr[k] = transposes(ps_pt[k % 2], srcs, c_tr)

        def tr_out(u, j):
            k = 5 * u + j
            t_plo[k] = hi_lo(ps_pt[k % 2][:, :], pth[:, k % 2], ptl[:, k % 2], t_tr[k], t_pv.get(k - 2),
                             c_phi, c_plo)

        def pv_pe(u, j):
            k, g = 5 * u + j, head(u) // 4
            b = g % 2
            pe.wait(t_plo[k], t_v[g], state.get("vn"))
            if j == 0:
                pe.wait(t_olo.get(u - 1))
            h, l = pth[:, k % 2], ptl[:, k % 2]
            if j < 4:
                terms = [(vh[:, b, j], h), (vl[:, b, j], h), (vh[:, b, j], l)]
            else:
                terms = [(v4a[:, b], h), (v4b[:, b], l)]
            t_pv[k] = products(ps_o, terms, c_pv, first=j == 0, final=j == 4)
            v_done[g] = t_pv[k]
            if j == 4:
                t_olo[u] = hi_lo(ps_o, oh[:, u % 3], ol[:, u % 3], t_pv[k], t_wod.get(u - 3), c_ohi, c_olo)

        def wo_pe(u, t):
            a, z, tt = 128 * t, 128 * t + 128, 4 * qg(u) + t
            pe.wait(t_olo[u], t_wo[head(u - 1)], t_wo[head(u)], m_free[0])
            terms = []
            for w in (u - 1, u):
                h = head(w)
                terms += split3(oh[:, w % 3, a:z], ol[:, w % 3, a:z], woh[:, h % 3], wol[:, h % 3])
            tok = products(ps_m, terms, c_wo)
            for w in (u - 1, u):
                t_wod[w] = tok
                wo_done[head(w)] = tok
            dve.wait(tok, t_addx[tt])
            m_free[0] = t_addx[tt] = dve.do(lambda e: e.tensor_tensor(
                xacc[:, tt, :], ps_m, xacc[:, tt, :], ALU.add), c_add)

        def score(u, t):
            if 0 <= u < UNITS:
                s_pe(u, t)
                s_max(u, t)
                s_exp(u, t)

        def norm(u, t):
            if 0 <= u < UNITS:
                s_norm(u, t)

        def turned(u, j):
            if 0 <= u < UNITS:
                tr_pe(u, j)
                tr_out(u, j)

        def value(u, j):
            if 0 <= u < UNITS:
                pv_pe(u, j)

        def project(u):
            if 0 <= u < UNITS:
                q_pe(u)

        def wo_steps(u, half):
            w = u - 1 if half == 0 else u - 2
            if w >= 1 and w % 2 == 1 and w < UNITS:
                return [(w, 2 * half), (w, 2 * half + 1)]
            return []

        def wo_run(lst, i):
            if i < len(lst):
                wo_pe(*lst[i])

        prefetch(1)
        project(0)
        for u in range(-1, UNITS + 2):
            todo = wo_steps(u, 0) + wo_steps(u, 1)
            prefetch(u + 2)
            score(u + 1, 0)
            turned(u, 0)
            norm(u + 1, 0)
            turned(u, 1)
            score(u + 1, 1)
            value(u, 0)
            wo_run(todo, 0)
            turned(u, 2)
            norm(u + 1, 1)
            score(u + 1, 2)
            value(u, 1)
            turned(u, 3)
            norm(u + 1, 2)
            score(u + 1, 3)
            value(u, 2)
            wo_run(todo, 1)
            turned(u, 4)
            norm(u + 1, 3)
            value(u, 3)
            project(u + 2)
            value(u, 4)
            for kind, n in plan.get(u, []):
                run_task(kind, n, pending.pop((kind, n)))

        def barrier():
            toks = [(c, c.n) for c in counts if c.n]
            for e in (pe, dve, act, pool, sp):
                e.wait(toks)

        counts = ([c_init, c_cst, c_xtr, c_xhi, c_xlo, c_gk, c_gv, c_wtr, c_whi, c_wlo, c_kv, c_kvd, c_kva, c_kvp, c_vn,
                   c_q, c_qhi, c_qlo, c_s, c_max, c_exp, c_rec, c_p, c_tr, c_phi, c_plo, c_pv, c_ohi, c_olo,
                   c_wo, c_add, c_ln, c_lna, c_bo, c_sub, c_sum, c_ff, c_ffa, c_ffd] + c_raw + c_x + c_ctx)
        barrier()
        one.close()

        two = ExitStack()
        HT = NT // 2
        x2h, x2l = pair("x2T", [128, NC, 1024], two)
        cth, ctl = pair("ctT", [128, NC, 1024], two)
        wh, wl = pair("xw", [128, 6, 512], two)
        uh, ul = pair("xwo", [128, 4, 512], two)
        raw2 = sb("raw2", [128, 4, 512], F32, two)
        rawc = sb("rawc", [128, 2, 512], F32, two)
        kh, kl = pair("xk", [128, 1024], two)
        v2h, v2l = pair("xv", [128, HT, 128], two)
        q2h, q2l = pair("xq", [128, 2, 8, 128], two)
        P2 = sb("P2", [128, 2, 512], F32, two)
        p2h, p2l = pair("xp", [128, 512], two)
        o2h, o2l = pair("xo", [128, 2, 2, 512], two)
        bob = sb("bob", [128, 512], F32, two)
        mx2 = sb("mx2", [128, 2, 8], F32, two)
        sm2 = sb("sm2", [128, 2, 8], F32, two)

        ps_q = [big[0][:, 0, :], big[0][:, 1, :]]
        ps_sc = bank[0]
        ps_tp = bank[1]
        ps_ov = [big[1][:, 0, :], big[1][:, 1, :]]
        ps_w = [big[2][:, 0, :], big[2][:, 1, :]]

        sp.do(lambda e: e.dma_start(bob[:, :], xbo.rearrange("(a d) -> a d", a=1).to_broadcast([128, 512])),
              c_cst, 16)
        sp.do(lambda e: e.dma_start(raw2[0:32, 3, 0:128], xbq.rearrange("(h d) -> h d", d=128)), c_cst, 16)
        t_b = sp.do(lambda e: e.dma_start(raw2[32:48, 3, 0:128], xbkv.rearrange("(h d) -> h d", d=128)), c_cst, 16)
        pe.wait(t_b)
        t = pe.do(lambda e: e.transpose(ps_sc[:, 0:48], raw2[0:48, 3, 0:128], ident[0:48, 0:48]), c_xtr)
        dve.wait(t)
        t_bqk = dve.do(lambda e: e.tensor_copy(bqk[:, :], ps_sc[:, 0:48]), c_kvd)

        raw2_free = [None, None, None, t]
        raw2_n = [0]

        def load2(src, blocks):
            s = raw2_n[0] % 4
            raw2_n[0] += 1
            sp.wait(raw2_free[s])
            dst = raw2[:, s, :].rearrange("p (o d) -> p o d", d=128) if blocks else raw2[:, s, :]
            return s, sp.do(lambda e: e.dma_start(dst, src), c_raw[s], 16)

        wq2_v = xWq.rearrange("(c p) (h d) -> h p c d", p=128, d=128)
        wkv2_v = xWkv.rearrange("(c p) (h d) -> h p c d", p=128, d=128)
        wo2_v = xWo.rearrange("(h p) n -> h p n", p=128)

        t_w, w_done = {}, {}

        def weight2(key, loaded, hi, lo, slot):
            s, t_in = loaded
            act.wait(t_in, w_done.get(slot))
            a = act.do(lambda e: e.activation(hi, raw2[:, s, :], ACT.Copy), c_whi)
            pool.wait(a)
            t_w[key] = raw2_free[s] = pool.do(lambda e: e.tensor_tensor(
                lo, raw2[:, s, :], f(hi), ALU.subtract), c_wlo)

        def w_slot(kind, n):
            if kind == "wk":
                return ("w", 0)
            if kind == "wv":
                return ("w", 1)
            if kind == "wq":
                return ("w", 2 + n % 4)
            return ("u", n % 4)

        def w_load(kind, n):
            if kind == "wk":
                return load2(wkv2_v[n], True)
            if kind == "wv":
                return load2(wkv2_v[G + n], True)
            if kind == "wq":
                return load2(wq2_v[n], True)
            return load2(wo2_v[n], False)

        def w_make(th, kind, n, loaded):
            which, s = w_slot(kind, n)
            hi, lo = (wh[:, s], wl[:, s]) if which == "w" else (uh[:, s], ul[:, s])
            weight2((th, kind, n), loaded, hi, lo, (which, s))

        def w_at(kind, n, c):
            _, s = w_slot(kind, n)
            return wh[:, s, 128 * c:128 * c + 128], wl[:, s, 128 * c:128 * c + 128]

        need = []
        for th in range(2):
            for g in range(G):
                need += [(th, "wk", g), (th, "wq", 4 * g), (th, "wq", 4 * g + 1), (th, "wv", g),
                         (th, "wo", 4 * g), (th, "wo", 4 * g + 1), (th, "wq", 4 * g + 2), (th, "wq", 4 * g + 3),
                         (th, "wo", 4 * g + 2), (th, "wo", 4 * g + 3)]
        fetched = []
        at = [0, 0]

        def w_fetch(n):
            while at[0] < min(n, len(need)):
                fetched.append(w_load(*need[at[0]][1:]))
                at[0] += 1

        def w_next(n):
            for _ in range(n):
                if at[1] < len(need):
                    w_fetch(at[1] + 3)
                    th, kind, k = need[at[1]]
                    w_make(th, kind, k, fetched[at[1]])
                    at[1] += 1

        rawc_free = [None, None]
        q_free = [None, None]
        q_turn = [0]
        k_free, v_free, sc_free, tp_free = [None], [None], [None], [None]
        p2_free, s2_free = [None], [None, None]
        ov_free, w_free = [None, None], [None, None]
        qslot_free, oslot_free = [None, None], [None, None]
        t2_q, t2_o, t2_k, t2_v = {}, {}, {}, {}
        w_turn = [0]
        t_x2 = [None] * NT
        t_ct = [None] * NT

        def ctx_tile(tt, cols):
            s = tt % 2
            sp.wait(rawc_free[s])
            t_in = sp.do(lambda e: e.dma_start(rawc[:, s, :], cf[128 * tt:128 * tt + 128, :]), c_ctx[s], 16)
            t, lo = transposed_tile(tt, [rawc[:, s, 128 * c:128 * c + 128] for c in range(NC)], t_in,
                                    cth, ctl, cols, xbanks)
            rawc_free[s] = t
            t_ct[tt] = lo

        def x2_tile(tt, cols, t_in):
            t, lo = transposed_tile(tt, [xacc[:, tt, 128 * c:128 * c + 128] for c in range(NC)], t_in,
                                    x2h, x2l, cols, xbanks)
            t_x2[tt] = lo
            pool.wait(t, t_b)
            t_addx[tt] = pool.do(lambda e: e.tensor_tensor(xacc[:, tt, :], xacc[:, tt, :], bob[:, :], ALU.add), c_bo)

        xbanks = [ps_tp[:, :], ps_w[0], ps_w[1], ps_ov[0], ps_ov[1]]
        for k in list(turn):
            if isinstance(k, tuple):
                turn.pop(k)
        turn["x"] = 0

        units = [(th, g, p, s) for th in range(2) for g in range(G) for p in range(2) for s in range(2)]

        def rows2(th, s):
            return list(range(HT * th + 4 * s, HT * th + 4 * s + 4))

        def qproj(n):
            th, g, p, s = units[n]
            pe.wait([t_x2[t] for t in rows2(th, s)], t_bqk)
            for j in range(2):
                h = 4 * g + 2 * p + j
                b = q_turn[0] % 2
                q_turn[0] += 1
                pe.wait(t_w[(th, "wq", h)], q_free[b])
                terms = []
                for c in range(NC):
                    terms += split3(*w_at("wq", h, c), x2h[:, c, 512 * s:512 * s + 512],
                                    x2l[:, c, 512 * s:512 * s + 512])
                t = products(ps_q[b], terms, c_q)
                w_done[w_slot("wq", h)] = t
                hi, lo = q2h[:, n % 2, :, 64 * j:64 * j + 64], q2l[:, n % 2, :, 64 * j:64 * j + 64]
                src = ps_q[b].rearrange("p (b i) -> p b i", i=64)
                act.wait(t, qslot_free[n % 2])
                a = act.do(lambda e, hi=hi, src=src, h=h: e.activation(
                    hi, src, ACT.Identity, bias=bqk[:, h:h + 1]), c_qhi)
                dve.wait(a)
                q_free[b] = t2_q[n] = dve.do(lambda e, hi=hi, lo=lo, src=src, h=h: e.scalar_tensor_tensor(
                    lo, src, bqk[:, h:h + 1], f(hi), ALU.add, ALU.subtract), c_qlo)

        def kproj(th, g):
            for s in range(2):
                b = q_turn[0] % 2
                q_turn[0] += 1
                pe.wait(t_w[(th, "wk", g)], [t_ct[t] for t in rows2(th, s)], q_free[b], t_bqk)
                terms = []
                for c in range(NC):
                    terms += split3(*w_at("wk", g, c), cth[:, c, 512 * s:512 * s + 512],
                                    ctl[:, c, 512 * s:512 * s + 512])
                t = products(ps_q[b], terms, c_kv)
                w_done[w_slot("wk", g)] = t
                hi, lo = kh[:, 512 * s:512 * s + 512], kl[:, 512 * s:512 * s + 512]
                act.wait(t, k_free[0])
                a = act.do(lambda e, hi=hi, b=b: e.activation(
                    hi, ps_q[b], ACT.Identity, bias=bqk[:, 32 + g:33 + g]), c_kva)
                dve.wait(a)
                q_free[b] = dve.do(lambda e, hi=hi, lo=lo, b=b: e.scalar_tensor_tensor(
                    lo, ps_q[b], bqk[:, 32 + g:33 + g], f(hi), ALU.add, ALU.subtract), c_kvd)
            t2_k[(th, g)] = q_free[b]

        def vproj(th, g):
            for s in range(2):
                b = q_turn[0] % 2
                q_turn[0] += 1
                pe.wait(t_w[(th, "wv", g)], [t_ct[t] for t in rows2(th, s)], q_free[b])
                for i in range(4):
                    a0 = 512 * s + 128 * i
                    terms = []
                    for c in range(NC):
                        terms += split3(cth[:, c, a0:a0 + 128], ctl[:, c, a0:a0 + 128], *w_at("wv", g, c))
                    t = products(ps_q[b][:, 128 * i:128 * i + 128], terms, c_kv)
                w_done[w_slot("wv", g)] = t
                q_free[b] = hi_lo(ps_q[b], flat(v2h[:, 4 * s:4 * s + 4, :]), flat(v2l[:, 4 * s:4 * s + 4, :]),
                                  t, v_free[0], c_kva, c_kvd)
            t2_v[(th, g)] = q_free[b]

        def scores2(n):
            th, g, p, s = units[n]
            pe.wait(t2_q[n], t2_k[(th, g)], sc_free[0])
            for b in range(8):
                qa = [v[:, n % 2, b, :] for v in (q2h, q2l)]
                a0 = 512 * s + 64 * b
                t = products(ps_sc[:, 64 * b:64 * b + 64],
                             split3(qa[0], qa[1], kh[:, a0:a0 + 64], kl[:, a0:a0 + 64]), c_s)
            qslot_free[n % 2] = t
            k_free[0] = t
            i = n % 2
            sv = ps_sc[:, :].rearrange("p (b k) -> p b k", k=64)
            pv = P2[:, i, :].rearrange("p (b k) -> p b k", k=64)
            dve.wait(t)
            m = dve.do(lambda e: e.tensor_reduce(mx2[:, i, :], sv, AX.X, ALU.max), c_max)
            dve.wait(m, s2_free[i])
            sc_free[0] = d = dve.do(lambda e: e.tensor_tensor(
                pv, sv, mx2[:, i, :].unsqueeze(2).to_broadcast([128, 8, 64]), ALU.subtract), c_sub)
            act.wait(d)
            x_ = act.do(lambda e: e.activation(P2[:, i, :], P2[:, i, :], ACT.Exp, scale=SCALE), c_exp)
            return x_

        def softmax2(n, x_):
            i = n % 2
            pv = P2[:, i, :].rearrange("p (b k) -> p b k", k=64)
            dve.wait(x_)
            a = dve.do(lambda e: e.tensor_reduce(sm2[:, i, :], pv, AX.X, ALU.add), c_sum)
            dve.wait(a)
            a = dve.do(lambda e: e.reciprocal(sm2[:, i, :], sm2[:, i, :]), c_rec)
            pool.wait(a)
            return pool.do(lambda e: e.tensor_tensor(
                pv, pv, sm2[:, i, :].unsqueeze(2).to_broadcast([128, 8, 64]), ALU.mult), c_p)

        def turn2(n, t_in):
            i = n % 2
            pe.wait(t_in, tp_free[0])
            t = transposes(ps_tp, [P2[:, i, 128 * b:128 * b + 128] for b in range(4)], c_tr)
            s2_free[i] = t
            tp_free[0] = hi_lo(ps_tp[:, :], p2h[:, :], p2l[:, :], t, p2_free[0], c_phi, c_plo)
            return tp_free[0]

        def values2(n, t_in):
            th, g, p, s = units[n]
            pe.wait(t_in, t2_v[(th, g)], ov_free[0], ov_free[1])
            for bp in range(4):
                for par in range(2):
                    r = slice(64 * par, 64 * par + 64)
                    cc = slice(128 * bp, 128 * bp + 128)
                    t = products(ps_ov[par][:, cc],
                                 split3(v2h[r, 4 * s + bp, :], v2l[r, 4 * s + bp, :], p2h[r, cc], p2l[r, cc]), c_pv)
            p2_free[0] = t
            v_free[0] = t
            o = n % 2
            bv = bqk[:, 40 + g:41 + g]
            act.wait(t, oslot_free[o], t_bqk)
            for par in range(2):
                views = []
                for j in range(2):
                    src = ps_ov[par].rearrange("p (b h i) -> p h b i", h=2, i=64)[:, j]
                    hi = o2h[:, o, j, :].rearrange("p (b a i) -> p a b i", a=2, i=64)[:, par]
                    lo = o2l[:, o, j, :].rearrange("p (b a i) -> p a b i", a=2, i=64)[:, par]
                    views.append((src, hi, lo))
                    a = act.do(lambda e, hi=hi, src=src: e.activation(hi, src, ACT.Identity, bias=bv), c_ohi)
                dve.wait(a)
                for src, hi, lo in views:
                    ov_free[par] = dve.do(lambda e, hi=hi, lo=lo, src=src: e.scalar_tensor_tensor(
                        lo, src, bv, f(hi), ALU.add, ALU.subtract), c_olo)
            t2_o[n] = ov_free[1]

        def wo2(n, tiles):
            if n < 0:
                return
            th, g, p, s = units[n]
            for t in tiles:
                tt = rows2(th, s)[t]
                b = w_turn[0] % 2
                w_turn[0] += 1
                hs = (4 * g + 2 * p, 4 * g + 2 * p + 1)
                pe.wait(t2_o[n], [t_w[(th, "wo", h)] for h in hs], w_free[b])
                terms = []
                for j, h in enumerate(hs):
                    terms += split3(o2h[:, n % 2, j, 128 * t:128 * t + 128], o2l[:, n % 2, j, 128 * t:128 * t + 128],
                                    uh[:, h % 4], ul[:, h % 4])
                tok = products(ps_w[b], terms, c_wo)
                for h in hs:
                    w_done[w_slot("wo", h)] = tok
                oslot_free[n % 2] = tok
                dve.wait(tok, t_addx[tt])
                w_free[b] = t_addx[tt] = dve.do(lambda e, b=b, tt=tt: e.tensor_tensor(
                    xacc[:, tt, :], ps_w[b], xacc[:, tt, :], ALU.add), c_add)

        t_ln = [layernorm(list(range(4 * q, 4 * q + 4)), [t_addx[t] for t in range(4 * q, 4 * q + 4)])
                for q in range(4)]

        for th in range(2):
            for i in range(HT):
                ctx_tile(HT * th + i, 128 * i)
            for i in range(HT):
                tt = HT * th + i
                x2_tile(tt, 128 * i, t_ln[tt // 4])
            base = 32 * th
            if th == 0:
                w_next(5)
            kproj(th, 0)
            qproj(base)
            vproj(th, 0)
            for n in range(base, base + 32):
                _, g, p, s = units[n]
                x_ = scores2(n)
                more = n + 1 < base + 32
                fresh = more and units[n + 1][1] != g
                if (p, s) in ((0, 0), (0, 1), (1, 0)):
                    w_next({(0, 0): 3, (0, 1): 2, (1, 0): 2}[(p, s)])
                else:
                    w_next(3)
                wo2(n - 1 if n > base else -1, (0,))
                t_p2 = softmax2(n, x_)
                if more:
                    qproj(n + 1)
                wo2(n - 1 if n > base else -1, (1,))
                t_t2 = turn2(n, t_p2)
                if fresh:
                    kproj(th, units[n + 1][1])
                wo2(n - 1 if n > base else -1, (2, 3))
                values2(n, t_t2)
                if fresh:
                    vproj(th, units[n + 1][1])
            wo2(base + 31, (0, 1, 2, 3))
            for k in list(turn):
                if isinstance(k, tuple):
                    turn[k] = [(c, c.n) for c in (c_olo, c_add, c_plo)]
        barrier()
        two.close()

        three = ExitStack()
        x3h, x3l = pair("x3T", [128, NC, T], three)
        fwh, fwl = pair("fwT", [128, NC, D], three)
        fah, fal = pair("fa", [128, NC, E_R], three)
        fbh, fbl = pair("fbm", [128, D], three)
        raw3 = sb("raw3", [128, 4, 512], F32, three)
        rawa = sb("rawa", [128, 4, 128], F32, three)
        rawb = sb("rawb", [128, 512], F32, three)
        fbb = sb("fbb", [128, 512], F32, three)
        uTh, uTl = pair("uT", [128, 512], three)
        z = sb("z", [128, 2, 512], F32, three)
        junk = sb("junk", [128, 512], F32, three)
        nrm = sb("nrm", [128, 4, 2], F32, three)
        nz = sb("nz", [128, 4, 2], F32, three)
        gam = sb("gam", [128, 4], F32, three)

        sp.do(lambda e: e.dma_start(raw3[:, :, :], fW.rearrange("(o p) d -> p o d", p=128)), c_cst, 16)
        sp.do(lambda e: e.dma_start(fbb[:, :], fb.rearrange("(a d) -> a d", a=1).to_broadcast([128, 512])), c_cst, 16)
        for c in range(NC):
            sp.do(lambda e, c=c: e.dma_start(
                rawa[:, c, :].rearrange("p (x r) -> p x r", r=16),
                fA[:, 128 * c:128 * c + 128, :].rearrange("x p r -> p x r")), c_cst, 16)
        sp.do(lambda e: e.dma_start(rawb[:, :], fB.rearrange("x r o -> (x r) o")), c_cst, 16)
        t_f = sp.do(lambda e: e.dma_start(
            pcol[:, :], fp.rearrange("(x o) -> x o", o=1).unsqueeze(1).to_broadcast([8, 16, 1]),
            allow_slow_non_contiguous=True), c_cst, 16)

        xbanks3 = [bank[0][:, :], bank[1][:, :]]
        for k in list(turn):
            if isinstance(k, tuple):
                turn.pop(k)
        turn["x"] = 0
        for o in range(4):
            _, t_fw = transposed_tile(o, [raw3[:, o, 128 * c:128 * c + 128] for c in range(NC)], t_f,
                                      fwh, fwl, 128 * o, xbanks3)
        act.wait(t_f)
        a = act.do(lambda e: e.activation(flat(fah[:, :, :]), flat(rawa[:, :, :]), ACT.Copy), c_ffa)
        dve.wait(a)
        dve.do(lambda e: e.tensor_tensor(flat(fal[:, :, :]), flat(rawa[:, :, :]), f(flat(fah[:, :, :])), ALU.subtract),
               c_ffd)
        a = act.do(lambda e: e.activation(fbh[:, :], rawb[:, :], ACT.Copy), c_ffa)
        dve.wait(a)
        t_fab = dve.do(lambda e: e.tensor_tensor(fbl[:, :], rawb[:, :], f(fbh[:, :]), ALU.subtract), c_ffd)

        t_ln3 = [layernorm(list(range(4 * q, 4 * q + 4)), [t_addx[t] for t in range(4 * q, 4 * q + 4)])
                 for q in range(4)]
        t_x3 = [None] * NT
        for tt in range(NT):
            _, t_x3[tt] = transposed_tile(tt, [xacc[:, tt, 128 * c:128 * c + 128] for c in range(NC)],
                                          t_ln3[tt // 4], x3h, x3l, 128 * tt, xbanks3)
        ps_u = big[0][:, 0, :]
        ps_z = [big[1][:, 0, :], big[1][:, 1, :]]
        ps_mm = [big[2][:, 0, :], big[2][:, 1, :]]
        z_free, mm_free, u_free, uslot = [None, None], [None, None], None, None
        t_zs = [None, None]
        gam_free = [None] * 4
        t_n = None
        for q in range(4):
            c0 = 512 * q
            pe.wait([t_x3[t] for t in range(4 * q, 4 * q + 4)], t_fab, t_fw, u_free)
            terms = []
            for c in range(NC):
                terms += split3(fah[:, c, :], fal[:, c, :], x3h[:, c, c0:c0 + 512], x3l[:, c, c0:c0 + 512])
            t = products(ps_u, terms, c_ff)
            act.wait(t, uslot)
            a = act.do(lambda e: e.activation(uTh[:, :], ps_u, ACT.Identity, scale=pcol[:, 0:1]), c_ffa)
            dve.wait(a)
            u_free = dve.do(lambda e: e.scalar_tensor_tensor(
                uTl[:, :], ps_u, pcol[:, 0:1], f(uTh[:, :]), ALU.mult, ALU.subtract), c_ffd)
            for i in range(4):
                tt = 4 * q + i
                b = tt % 2
                s = slice(128 * tt, 128 * tt + 128)
                us = slice(128 * i, 128 * i + 128)
                pe.wait(z_free[b])
                terms = []
                for c in range(NC):
                    terms += split3(x3h[:, c, s], x3l[:, c, s], fwh[:, c, :], fwl[:, c, :])
                t_z = products(ps_z[b], terms, c_ff)
                pe.wait(u_free, mm_free[b])
                t_m = products(ps_mm[b], split3(uTh[:, us], uTl[:, us], fbh[:, :], fbl[:, :]), c_ff)
                uslot = t_m
                dve.wait(t_z, t_zs[b])
                z_free[b] = t_zz = dve.do(lambda e, b=b: e.tensor_tensor(z[:, b, :], ps_z[b], fbb[:, :], ALU.add),
                                          c_ffd)
                act.wait(t_zz, t_n)
                a = act.do(lambda e, b=b, i=i: e.activation(junk[:, :], z[:, b, :], ACT.Square,
                                                            accum_out=nrm[:, i, 0:1]), c_ffa)
                act.wait(t_m, a)
                a = act.do(lambda e, b=b, i=i: e.activation(junk[:, :], ps_mm[b], ACT.Square,
                                                            accum_out=nrm[:, i, 1:2]), c_ffa)
                act.wait(a)
                a = act.do(lambda e, i=i: e.activation(nz[:, i, :], nrm[:, i, :], ACT.Sqrt), c_ffa)
                t_n = a
                dve.wait(a)
                d = dve.do(lambda e, i=i: e.tensor_scalar(nz[:, i, 1:2], nz[:, i, 1:2], 1e-6, None, ALU.add), c_ffd)
                dve.wait(d)
                d = dve.do(lambda e, i=i: e.reciprocal(nz[:, i, 1:2], nz[:, i, 1:2]), c_ffd)
                dve.wait(d)
                d = dve.do(lambda e, i=i: e.scalar_tensor_tensor(
                    gam[:, i:i + 1], nz[:, i, 0:1], 0.5, nz[:, i, 1:2], ALU.mult, ALU.mult), c_ffd)
                dve.wait(d)
                d = dve.do(lambda e, i=i: e.tensor_scalar(gam[:, i:i + 1], gam[:, i:i + 1], 1.0, None, ALU.min), c_ffd)
                dve.wait(d)
                d = dve.do(lambda e, b=b, i=i: e.scalar_tensor_tensor(
                    z[:, b, :], ps_mm[b], gam[:, i:i + 1], z[:, b, :], ALU.mult, ALU.add), c_ffd)
                mm_free[b] = d
                dve.wait(d, t_x3[tt])
                t_zs[b] = t_addx[tt] = dve.do(lambda e, b=b, tt=tt: e.tensor_tensor(
                    xacc[:, tt, :], xacc[:, tt, :], z[:, b, :], ALU.add), c_add)
            t_l = layernorm(list(range(4 * q, 4 * q + 4)), [t_addx[4 * q + 3]])
            sp.wait(t_l)
            t_out = sp.do(lambda e, c0=c0, q=q: e.dma_start(
                of[c0:c0 + 512, :].rearrange("(t p) d -> p t d", p=128), xacc[:, 4 * q:4 * q + 4, :]), c_out, 16)
        sp.wait(t_out)
        three.close()

        block = top.enter_context(nc.Block())

        @block.sync
        def _(e):
            sp.run(e)

        @block.gpsimd
        def _(e):
            pool.run(e)

        @block.scalar
        def _(e):
            act.run(e)

        @block.vector
        def _(e):
            dve.run(e)

        @block.tensor
        def _(e):
            pe.run(e)


_INS = ['x', 'ctx_4096', 'L0_attn_freqs_cos', 'L0_attn_freqs_sin', 'L0_attn_wq', 'L0_attn_wk', 'L0_attn_wv',
        'L0_attn_wo', 'L0_attn_k_cache', 'L0_attn_v_cache', 'L0_attn_block_idx', 'L0_xattn_Wq', 'L0_xattn_bq',
        'L0_xattn_Wkv', 'L0_xattn_bkv', 'L0_xattn_Wo', 'L0_xattn_bo', 'L0_ffn_W', 'L0_ffn_b', 'L0_ffn_A',
        'L0_ffn_B', 'L0_ffn_p_scores']


def kernel(**inputs):
    import numpy as np
    import concourse.bacc as bacc
    from concourse.bass_utils import run_bass_kernel_spmd as run

    nc = bacc.Bacc("TRN2", target_bir_lowering=False, num_devices=1)
    arrays, args = {}, []
    for name in _INS:
        a = np.ascontiguousarray(inputs[name])
        arrays[f"in_{name}"] = a
        args.append(nc.dram_tensor(f"in_{name}", a.shape, mybir.dt.from_np(a.dtype), kind="ExternalInput").ap())
    o = nc.dram_tensor("out_0", (32, 64, 512), F32, kind="ExternalOutput").ap()
    decoder_kernel(nc, *args, o)
    r = run(nc, [arrays], core_ids=[0])
    return r.results[0]["out_0"]
```

```python
import concourse.bass as bass
from concourse import mybir
from contextlib import ExitStack

F32 = mybir.dt.float32
F32R = mybir.dt.float32r
I32 = mybir.dt.int32
U32 = mybir.dt.uint32
ALU = mybir.AluOpType
ACT = mybir.ActivationFunctionType
AX = mybir.AxisListType

D = 512
T = 2048
NT = T // 128
NC = D // 128
NH = 32
G = 8
HD = 128
KEYS = 576
HALF = KEYS // 2
SCALE = float(HD) ** -0.5
LN_EPS = 1e-5
E_R = 128


class Count:

    def __init__(self, h):
        self.h, self.n = h, 0


class Queue:

    def __init__(self):
        self.ops, self.seen = [], {}

    def wait(self, *tokens):
        for t in tokens:
            if t is None:
                continue
            if isinstance(t, list):
                self.wait(*t)
                continue
            c, v = t
            if self.seen.get(id(c), 0) < v:
                self.seen[id(c)] = v
                self.ops.append(lambda e, h=c.h, v=v: e.wait_ge(h, v))

    def do(self, fn, count=None, by=1):
        if count is None:
            self.ops.append(fn)
            return None
        self.ops.append(lambda e: fn(e).then_inc(count.h, by))
        count.n += by
        return (count, count.n)

    def run(self, e):
        for op in self.ops:
            op(e)


def decoder_kernel(nc, x, ctx_in, fcos, fsin, wq, wk, wv, wo, k_cache, v_cache, block_idx,
                   xWq, xbq, xWkv, xbkv, xWo, xbo, fW, fb, fA, fB, fp, out):
    with ExitStack() as top:
        pe, dve, act, pool, sp = Queue(), Queue(), Queue(), Queue(), Queue()

        def sem(name):
            return Count(top.enter_context(nc.semaphore(name)))

        def sb(name, shape, dt=F32, scope=top):
            return scope.enter_context(nc.sbuf_tensor(name, shape, dt))

        def pair(name, shape, scope=top):
            return sb(name + "h", shape, F32R, scope), sb(name + "l", shape, F32R, scope)

        def f(ap):
            return ap.bitcast(F32)

        xf = x.rearrange("a b d -> (a b) d")
        cf = ctx_in.rearrange("a b d -> (a b) d")
        of = out.rearrange("a b d -> (a b) d")

        bank = [top.enter_context(nc.psum_tensor(f"bank{i}", [128, 512], F32)) for i in range(2)]
        big = [top.enter_context(nc.psum_tensor(f"big{i}", [128, 2, 512], F32)) for i in range(3)]
        ps_pt = [bank[0], bank[1]]
        ps_s = [big[0], big[1]]
        ps_o = big[2][:, 0, :]
        ps_m = big[2][:, 1, :]

        c_init = sem("c_init")
        c_x = [sem(f"c_x{i}") for i in range(4)]
        c_cst = sem("c_cst")
        c_xtr = sem("c_xtr")
        c_xhi = sem("c_xhi")
        c_xlo = sem("c_xlo")
        c_raw = [sem(f"c_raw{i}") for i in range(4)]
        c_gk = sem("c_gk")
        c_gv = sem("c_gv")
        c_wtr = sem("c_wtr")
        c_whi = sem("c_whi")
        c_wlo = sem("c_wlo")
        c_kv = sem("c_kv")
        c_kvd = sem("c_kvd")
        c_kva = sem("c_kva")
        c_kvp = sem("c_kvp")
        c_vn = sem("c_vn")
        c_q = sem("c_q")
        c_qhi = sem("c_qhi")
        c_qlo = sem("c_qlo")
        c_s = sem("c_s")
        c_max = sem("c_max")
        c_exp = sem("c_exp")
        c_rec = sem("c_rec")
        c_p = sem("c_p")
        c_tr = sem("c_tr")
        c_phi = sem("c_phi")
        c_plo = sem("c_plo")
        c_pv = sem("c_pv")
        c_ohi = sem("c_ohi")
        c_olo = sem("c_olo")
        c_wo = sem("c_wo")
        c_add = sem("c_add")
        c_ln = sem("c_ln")
        c_lna = sem("c_lna")
        c_bo = sem("c_bo")
        c_sub = sem("c_sub")
        c_sub2 = sem("c_sub2")
        c_sum = sem("c_sum")
        c_ff = sem("c_ff")
        c_ffa = sem("c_ffa")
        c_ffd = sem("c_ffd")
        c_out = sem("c_out")

        ident = sb("ident", [128, 128])
        xacc = sb("xacc", [128, NT, D])
        stat = sb("stat", [128, NT, 6])
        mv = sb("mv", [128, NT, 2])
        rstd = sb("rstd", [128, NT])
        bqk = sb("bqk", [128, 48])
        pcol = sb("pcol", [128, 1])

        t_id0 = pool.do(lambda e: e.memset(ident[:, :], 0.0), c_init)
        pool.wait(t_id0)
        t_id = pool.do(lambda e: e.affine_select(
            out=ident[:, :], in_=ident[:, :], compare_op=ALU.not_equal, fill=1.0, base=0,
            pattern=[[-1, 128]], channel_multiplier=1), c_init)

        t_x = []
        for q in range(4):
            t_x.append(sp.do(lambda e, q=q: e.dma_start(
                xacc[:, 4 * q:4 * q + 4, :],
                xf[512 * q:512 * q + 512, :].rearrange("(t p) d -> p t d", p=128)), c_x[q], 16))

        def products(dst, terms, count, first=True, final=True):
            tok = None
            for i, (a, b) in enumerate(terms):
                end = i == len(terms) - 1
                tok = pe.do(lambda e, a=a, b=b, s=first and i == 0, z=final and end:
                            e.matmul(dst, a, b, start=s, stop=z), count if end else None)
            return tok

        def split3(ah, al, bh, bl):
            return [(ah, bh), (ah, bl), (al, bh)]

        def transposes(dst, srcs, count):
            tok = None
            for i, s in enumerate(srcs):
                tok = pe.do(lambda e, i=i, s=s: e.transpose(dst[:, 128 * i:128 * i + 128], s, ident[:, :]),
                            count if i == len(srcs) - 1 else None)
            return tok

        def hi_lo(src, hi, lo, t_src, t_free, c_hi, c_lo):
            act.wait(t_src, t_free)
            a = act.do(lambda e: e.activation(hi, src, ACT.Copy), c_hi)
            dve.wait(a)
            return dve.do(lambda e: e.tensor_tensor(lo, src, f(hi), ALU.subtract), c_lo)

        turn = {}

        def transposed_tile(tt, srcs, t_srcs, hT, lT, col, banks):
            k = turn.setdefault("x", 0)
            turn["x"] += 1
            dst = banks[k % len(banks)]
            pe.wait(t_srcs, t_id, turn.get(("x", k % len(banks))))
            t = transposes(dst, srcs, c_xtr)
            v = dst.rearrange("p (c t) -> p c t", c=NC)
            lo = hi_lo(v, hT[:, :, col:col + 128], lT[:, :, col:col + 128], t, None, c_xhi, c_xlo)
            turn[("x", k % len(banks))] = lo
            return t, lo

        def layernorm(tiles, t_in):
            a, b = tiles[0], tiles[-1] + 1
            dve.wait(t_in)
            for tt in tiles:
                t = dve.do(lambda e, tt=tt: e.bn_stats(stat[:, tt, :], xacc[:, tt, :]), c_ln)
            dve.wait(t)
            for tt in tiles:
                t = dve.do(lambda e, tt=tt: e.bn_aggr(mv[:, tt, :], stat[:, tt, :]), c_ln)
            dve.wait(t)
            t = dve.do(lambda e: e.tensor_scalar(mv[:, a:b, 1], mv[:, a:b, 1], LN_EPS, None, ALU.add), c_ln)
            act.wait(t)
            t = act.do(lambda e: e.activation(rstd[:, a:b], mv[:, a:b, 1], ACT.Sqrt), c_lna)
            dve.wait(t)
            t = dve.do(lambda e: e.reciprocal(rstd[:, a:b], rstd[:, a:b]), c_ln)
            dve.wait(t)
            for tt in tiles:
                t = dve.do(lambda e, tt=tt: e.tensor_scalar(
                    xacc[:, tt, :], xacc[:, tt, :], mv[:, tt, 0:1], rstd[:, tt:tt + 1],
                    ALU.subtract, ALU.mult), c_ln)
            return t

        one = ExitStack()
        xTh, xTl = pair("xT", [128, NC, T], one)
        wqh, wql = pair("wqT", [128, 4, NC, 128], one)
        woh, wol = pair("woT", [128, 3, D], one)
        wkvh, wkvl = pair("wkvT", [128, NC, 128], one)
        raw = sb("raw", [128, 3, 512], F32, one)
        rkv = sb("rkv", [128, 4, 128], F32, one)
        krot = sb("krot", [128, 4, 128], F32, one)
        kTh, kTl = pair("kT", [128, 2, KEYS], one)
        vh, vl = pair("v", [128, 2, 4, 128], one)
        v4a, v4b = sb("v4a", [128, 2, 128], F32R, one), sb("v4b", [128, 2, 128], F32R, one)
        vtmp = sb("vtmp", [64, 128], F32R, one)
        P = sb("P", [128, 8, KEYS + 64], F32, one)
        pth, ptl = pair("pt", [128, 2, 512], one)
        qTh, qTl = pair("qT", [128, 2, 512], one)
        oh, ol = pair("oT", [128, 3, 512], one)
        cosb = sb("cosb", [128, 64], F32, one)
        sinb = sb("sinb", [128, 64], F32, one)
        ccol = sb("ccol", [128, 2], F32, one)
        cs2 = sb("cs2", [128, 1], F32, one)
        bidx = sb("bidx", [128, 4], I32, one)
        prow = sb("prow", [128, 1], I32, one)
        prowf = sb("prowf", [128, 1], F32, one)
        idx0 = sb("idx0", [128, 4], F32, one)
        idx = sb("idx", [128, G, 4], I32, one)
        nmx = sb("nmx", [128, 8], F32, one)
        rsum = sb("rsum", [128, 8], F32, one)
        rrec = sb("rrec", [128, 8], F32, one)

        bi = block_idx.rearrange("(k a) -> a k", a=4)
        for a in range(4):
            t_c = sp.do(lambda e, a=a: e.dma_start(
                bidx[32 * a:32 * a + 32, :], bi[a:a + 1, :].to_broadcast([32, 4]), allow_slow_non_contiguous=True), c_cst, 16)
        sp.do(lambda e: e.dma_start(cosb[:, :], fcos.to_broadcast([128, 64])), c_cst, 16)
        sp.do(lambda e: e.dma_start(sinb[:, :], fsin.to_broadcast([128, 64])), c_cst, 16)
        for i, v in enumerate((fcos, fsin)):
            t_c = sp.do(lambda e, i=i, v=v: e.dma_start(
                ccol[:, i:i + 1], v.rearrange("a (d o) -> (a d) o", o=1).unsqueeze(1).to_broadcast([64, 2, 1]),
                allow_slow_non_contiguous=True),
                c_cst, 16)
        t_row = t_id
        for a in range(4):
            pool.wait(t_row)
            t_row = pool.do(lambda e, a=a: e.iota(prow[32 * a:32 * a + 32, :], [[0, 1]], base=0,
                                                  channel_multiplier=8), c_init)
        dve.wait(t_c, t_row)
        t = dve.do(lambda e: e.tensor_copy(prowf[:, :], prow[:, :]), c_kvd)
        dve.wait(t)
        t = dve.do(lambda e: e.tensor_scalar(idx0[:, :], bidx[:, :], 256.0, prowf[:, 0:1], ALU.mult, ALU.add), c_kvd)
        dve.wait(t)
        for g in range(G):
            t_idx = dve.do(lambda e, g=g: e.tensor_scalar(idx[:, g, :], idx0[:, :], float(g), None, ALU.add), c_kvd)
        t = dve.do(lambda e: e.tensor_scalar(cosb[:, :], cosb[:, :], SCALE, None, ALU.mult), c_kvd)
        t = dve.do(lambda e: e.tensor_scalar(sinb[:, :], sinb[:, :], SCALE, None, ALU.mult), c_kvd)
        t = dve.do(lambda e: e.tensor_tensor(ccol[:, :], ccol[:, :], ccol[:, :], ALU.mult), c_kvd)
        dve.wait(t)
        t = dve.do(lambda e: e.tensor_tensor(cs2[:, :], ccol[:, 0:1], ccol[:, 1:2], ALU.add), c_kvd)
        dve.wait(t)
        t_rot = dve.do(lambda e: e.tensor_scalar(cs2[:, :], cs2[:, :], SCALE, None, ALU.mult), c_kvd)
        t_v4 = t_row
        for b in range(2):
            pool.wait(t_v4)
            t_v4 = pool.do(lambda e, b=b: e.memset(f(v4b[64:128, b, :]), 0.0), c_init)

        kc_v = k_cache.rearrange("n b h d -> (n b h) d")
        vc_v = v_cache.rearrange("n b h d -> (n b h) d")
        wq_v = wq.rearrange("(h p) d -> h p d", p=128)
        wk_v = wk.rearrange("(h p) d -> h p d", p=128)
        wv_v = wv.rearrange("(h p) d -> h p d", p=128)
        wo_v = wo.rearrange("(o p) (h d) -> h p o d", p=128, d=128)

        raw_free = [None] * 3
        raw_n = [0]

        def load_raw(dst_view, src):
            s = raw_n[0] % 3
            raw_n[0] += 1
            sp.wait(raw_free[s])
            return s, sp.do(lambda e: e.dma_start(dst_view(raw[:, s, :]), src), c_raw[s], 16)

        def as_rows(r):
            return r

        def as_blocks(r):
            return r.rearrange("p (o d) -> p o d", d=128)

        m_free = [None]
        pt_free, pt_n = [None, None], [0]

        def pt_bank():
            b = pt_n[0] % 2
            pt_n[0] += 1
            pe.wait(pt_free[b])
            return b, ps_pt[b][:, :]

        def weight(loaded, hi, lo, t_free):
            s, t_in = loaded
            b, ps = pt_bank()
            pe.wait(t_in, t_id)
            t = transposes(ps, [raw[:, s, 128 * c:128 * c + 128] for c in range(4)], c_wtr)
            raw_free[s] = t
            pt_free[b] = hi_lo(ps, hi, lo, t, t_free, c_whi, c_wlo)
            return pt_free[b]

        t_wq, t_wo, t_kT, t_v = {}, {}, {}, {}
        wq_done, wo_done = {}, {}
        k_done, v_done = {}, {}
        t_xT = [None] * 4
        state = {}

        def flat(ap):
            return ap.rearrange("p c d -> p (c d)")

        def gather(g, what, dst, src, count, t_free):
            pool.wait(t_idx, t_free)
            for b in range(4):
                t = pool.do(lambda e, b=b: e.indirect_dma_start(
                    dst[:, b, :], None, src, bass.IndirectOffsetOnAxis(ap=idx[:, g, b:b + 1].bitcast(U32), axis=0)),
                    count, 16)
            state[what] = t

        def task(kind, n):
            if kind == "wq":
                return ("wq", n, lambda: load_raw(as_rows, wq_v[n]))
            if kind == "wo":
                return ("wo", n, lambda: load_raw(as_blocks, wo_v[n]))
            if kind == "wk":
                return ("wk", n, lambda: load_raw(as_rows, wk_v[n]))
            if kind == "wv":
                return ("wv", n, lambda: load_raw(as_rows, wv_v[n]))
            return (kind, n, lambda: None)

        def run_task(kind, n, loaded):
            if kind == "wq":
                t_wq[n] = weight(loaded, flat(wqh[:, n % 4]), flat(wql[:, n % 4]), wq_done.get(n - 4))
            elif kind == "wo":
                t_wo[n] = weight(loaded, woh[:, n % 3], wol[:, n % 3], wo_done.get(n - 3))
            elif kind in ("wk", "wv"):
                state[kind] = weight(loaded, flat(wkvh[:, :, :]), flat(wkvl[:, :, :]), state.get("wkv_done"))
            elif kind == "gk":
                gather(n, "gk", rkv, kc_v, c_gk, state.get("rkv_done"))
            elif kind == "gv":
                gather(n, "gv", rkv, vc_v, c_gv, state.get("rkv_done"))
            elif kind == "rot":
                b = n % 2
                dve.wait(state["gk"], t_rot, state.get("krot_done"))
                src = rkv[:, :, :].rearrange("p b (d o) -> p b d o", o=2)
                dst = krot[:, :, :].rearrange("p b (d o) -> p b d o", o=2)
                cb = cosb[:, :].unsqueeze(1).to_broadcast([128, 4, 64])
                sn = sinb[:, :].unsqueeze(1).to_broadcast([128, 4, 64])
                for o in range(2):
                    t = dve.do(lambda e, o=o: e.tensor_tensor(dst[:, :, :, o], src[:, :, :, o], cb, ALU.mult), c_kvd)
                dve.wait(t)
                for o in range(2):
                    t = dve.do(lambda e, o=o: e.tensor_tensor(src[:, :, :, o], src[:, :, :, o], sn, ALU.mult), c_kvd)
                dve.wait(t)
                dve.do(lambda e: e.tensor_tensor(dst[:, :, :, 0], dst[:, :, :, 0], src[:, :, :, 1], ALU.add), c_kvd)
                t = dve.do(lambda e: e.tensor_tensor(dst[:, :, :, 1], dst[:, :, :, 1], src[:, :, :, 0], ALU.subtract),
                           c_kvd)
                state["rot"] = t
                state["rkv_done"] = t
            elif kind == "kT":
                b = n % 2
                w, ps = pt_bank()
                pe.wait(state["rot"], t_id)
                t = transposes(ps, [krot[:, j, :] for j in range(4)], c_kv)
                state["krot_done"] = t
                t_kT[n] = pt_free[w] = hi_lo(ps, kTh[:, b, 0:512], kTl[:, b, 0:512], t, k_done.get(n - 2),
                                            c_kva, c_kvd)
            elif kind == "kn":
                b = n % 2
                w, ps = pt_bank()
                pe.wait(state["wk"], t_xT[0])
                terms = []
                for c in range(NC):
                    terms += split3(wkvh[:, c, :], wkvl[:, c, :], xTh[:, c, 0:64], xTl[:, c, 0:64])
                t = products(ps[:, 0:64], terms, c_kv)
                state["wkv_done"] = t
                act.wait(t, t_rot, k_done.get(n - 2))
                hi, lo = kTh[:, b, 512:576], kTl[:, b, 512:576]
                a = act.do(lambda e: e.activation(hi, ps[:, 0:64], ACT.Identity, scale=cs2[:, 0:1]), c_kva)
                dve.wait(a)
                pt_free[w] = dve.do(lambda e: e.scalar_tensor_tensor(
                    lo, ps[:, 0:64], cs2[:, 0:1], f(hi), ALU.mult, ALU.subtract), c_kvd)
                state["kn"] = pt_free[w]
            elif kind == "vn":
                b = n % 2
                w, ps = pt_bank()
                pe.wait(state["wv"], t_xT[0])
                terms = []
                for c in range(NC):
                    terms += split3(xTh[:, c, 0:64], xTl[:, c, 0:64], wkvh[:, c, :], wkvl[:, c, :])
                t = products(ps[0:64, 0:128], terms, c_kv)
                state["wkv_done"] = t
                act.wait(t, v_done.get(n - 2), t_v4)
                act.do(lambda e: e.activation(v4a[0:64, b, :], ps[0:64, 0:128], ACT.Copy))
                a = act.do(lambda e: e.activation(v4b[0:64, b, :], ps[0:64, 0:128], ACT.Copy), c_kva)
                dve.wait(a, state.get("vn"))
                pt_free[w] = d = dve.do(lambda e: e.tensor_tensor(
                    vtmp[:, :], ps[0:64, 0:128], f(v4b[0:64, b, :]), ALU.subtract), c_kvd)
                sp.wait(d, v_done.get(n - 2))
                state["vn"] = sp.do(lambda e: e.dma_start(f(v4a[64:128, b, :]), f(vtmp[:, :])), c_vn, 16)
            elif kind == "vs":
                b = n % 2
                act.wait(state["gv"], v_done.get(n - 2))
                a = act.do(lambda e: e.activation(vh[:, b], rkv[:, :, :], ACT.Copy), c_kva)
                pool.wait(a)
                t = pool.do(lambda e: e.tensor_tensor(vl[:, b], rkv[:, :, :], f(vh[:, b]), ALU.subtract), c_kvp)
                state["rkv_done"] = t
                t_v[n] = [t]


        run_task("gk", 0, None)
        banks = [ps_o, ps_m, big[0][:, 0, :], big[0][:, 1, :], big[1][:, 0, :], big[1][:, 1, :]]
        pre = [task(*a) for a in (("wk", 0), ("wq", 0), ("wq", 1))]
        loads = [p[2]() for p in pre]
        for q in range(4):
            for tt in range(4 * q, 4 * q + 4):
                _, t_xT[q] = transposed_tile(tt, [xacc[:, tt, 128 * c:128 * c + 128] for c in range(NC)],
                                             t_x[q], xTh, xTl, 128 * tt, banks)
        t_pro = t_xT[3]
        run_task("wk", 0, loads[0])
        run_task("rot", 0, None)
        run_task("kn", 0, None)
        run_task("kT", 0, None)
        run_task("wq", 0, loads[1])
        run_task("wq", 1, loads[2])
        run_task("gv", 0, None)
        run_task("wv", 0, task("wv", 0)[2]())
        run_task("vn", 0, None)
        run_task("vs", 0, None)

        plan = {}
        for g in range(G):
            s = 16 * g
            plan[s] = [("wo", 4 * g)]
            plan[s + 1] = [("wo", 4 * g + 1)]
            plan[s + 2] = [("wq", 4 * g + 2)]
            plan[s + 3] = [("wq", 4 * g + 3)]
            plan[s + 8] = [("wo", 4 * g + 2)]
            plan[s + 9] = [("wo", 4 * g + 3)]
            if g + 1 < G:
                plan[s + 4] = [("gk", g + 1), ("wk", g + 1)]
                plan[s + 5] = [("rot", g + 1), ("kn", g + 1), ("gv", g + 1)]
                plan[s + 6] = [("kT", g + 1)]
                plan[s + 7] = [("vs", g + 1)]
                plan[s + 10] = [("wv", g + 1)]
                plan[s + 11] = [("vn", g + 1)]
                plan[s + 12] = [("wq", 4 * g + 4)]
                plan[s + 13] = [("wq", 4 * g + 5)]
        order = [(s, a) for s in sorted(plan) for a in plan[s]]
        queue = [(s, task(*a)) for s, a in order]
        pending = {}
        nxt = [0]

        def prefetch(upto):
            while nxt[0] < len(queue) and queue[nxt[0]][0] <= upto:
                s, (kind, n, load) = queue[nxt[0]]
                pending[(kind, n)] = load()
                nxt[0] += 1

        UNITS = 128
        t_qp, t_q, t_s, t_max, t_exp, t_rec, t_p = {}, {}, {}, {}, {}, {}, {}
        t_phi, t_bank = {}, {}
        t_tr, t_plo, t_pv, t_olo, t_wod = {}, {}, {}, {}, {}
        t_addx = [t_pro] * NT
        t_wop = {}

        def head(u):
            return 2 * (u // 8) + u % 2

        def qg(u):
            return (u % 8) // 2

        def q_pe(u, part):
            h, c0 = head(u), 512 * qg(u)
            if part == 0:
                pe.wait(t_wq[h], t_xT[qg(u)], m_free[0])
            terms = []
            for c in range(NC):
                terms += split3(wqh[:, h % 4, c, :], wql[:, h % 4, c, :],
                                xTh[:, c, c0:c0 + 512], xTl[:, c, c0:c0 + 512])
            if part == 0:
                products(ps_m, terms[:8], None, final=False)
            else:
                wq_done[h] = t_qp[u] = products(ps_m, terms[8:], c_q, first=False)

        def q_out(u):
            t_q[u] = hi_lo(ps_m, qTh[:, u % 2], qTl[:, u % 2], t_qp[u], t_s.get(4 * (u - 2) + 3), c_qhi, c_qlo)
            m_free[0] = t_q[u]

        def s_pe(u, t):
            i, b = 4 * u + t, (head(u) // 4) % 2
            pe.wait(t_q[u], t_kT[head(u) // 4], state.get("kn"), t_exp.get(i - 2))
            a, z = 128 * t, 128 * t + 128
            dst = ps_s[i % 2]
            terms = split3(qTh[:, u % 2, a:z], qTl[:, u % 2, a:z], kTh[:, b], kTl[:, b])
            for n, (l, r) in enumerate(terms):
                for k in range(2):
                    last = n == 2 and k == 1
                    tok = pe.do(lambda e, l=l, r=r, k=k, n=n: e.matmul(
                        dst[:, k, 0:HALF], l, r[:, HALF * k:HALF * k + HALF], start=n == 0, stop=n == 2),
                        c_s if last else None)
            t_s[i] = tok
            k_done[head(u) // 4] = tok

        def s_max(u, t):
            i = 4 * u + t
            dve.wait(t_s[i])
            t_max[i] = dve.do(lambda e: e.tensor_reduce(
                nmx[:, i % 8:i % 8 + 1], ps_s[i % 2][:, :, 0:HALF], AX.XY, ALU.max, negate=True), c_max)

        def s_exp(u, t):
            i = 4 * u + t
            act.wait(t_max[i], t_tr.get(5 * (u - 2) + 4))
            t_exp[i] = act.do(lambda e: e.activation(
                P[:, i % 8, 0:KEYS].rearrange("p (k n) -> p k n", k=2), ps_s[i % 2][:, :, 0:HALF], ACT.Exp,
                bias=nmx[:, i % 8:i % 8 + 1], scale=1.0, accum_out=rsum[:, i % 8:i % 8 + 1]), c_exp)

        def s_norm(u, t):
            i = 4 * u + t
            dve.wait(t_exp[i])
            t_rec[i] = dve.do(lambda e: e.reciprocal(rrec[:, i % 8:i % 8 + 1], rsum[:, i % 8:i % 8 + 1]), c_rec)
            pool.wait(t_rec[i])
            d = pool.do(lambda e: e.tensor_scalar(
                P[:, i % 8, KEYS:KEYS + 64], P[:, i % 8, 512:KEYS], rrec[:, i % 8:i % 8 + 1], 1.0,
                ALU.mult, ALU.mult), c_p)
            pool.wait(d)
            t_p[i] = pool.do(lambda e: e.tensor_scalar(
                P[:, i % 8, 0:KEYS], P[:, i % 8, 0:KEYS], rrec[:, i % 8:i % 8 + 1], 1.0, ALU.mult, ALU.mult), c_p)

        def tr_pe(u, j):
            k = 5 * u + j
            b, ps = pt_bank()
            t_bank[k] = b
            pe.wait(t_p[4 * u + 3])
            srcs = []
            for t in range(4):
                r = P[:, (4 * u + t) % 8, :]
                srcs.append(r[:, 128 * j:128 * j + 128])
            t_tr[k] = transposes(ps, srcs, c_tr)

        def tr_hi(u, j):
            k = 5 * u + j
            act.wait(t_tr[k], t_pv.get(k - 2))
            t_phi[k] = act.do(lambda e: e.activation(pth[:, k % 2], ps_pt[t_bank[k]][:, :], ACT.Copy), c_phi)

        def tr_lo(u, j):
            k = 5 * u + j
            dve.wait(t_phi[k])
            t_plo[k] = pt_free[t_bank[k]] = dve.do(lambda e: e.tensor_tensor(
                ptl[:, k % 2], ps_pt[t_bank[k]][:, :], f(pth[:, k % 2]), ALU.subtract), c_plo)

        def pv_pe(u, j):
            k, g = 5 * u + j, head(u) // 4
            b = g % 2
            pe.wait(t_plo[k], t_v[g], state.get("vn"))
            if j == 0:
                pe.wait(t_olo.get(u - 1))
            h, l = pth[:, k % 2], ptl[:, k % 2]
            if j < 4:
                terms = [(vh[:, b, j], h), (vl[:, b, j], h), (vh[:, b, j], l)]
            else:
                terms = [(v4a[:, b], h), (v4b[:, b], l)]
            t_pv[k] = products(ps_o, terms, c_pv, first=j == 0, final=j == 4)
            v_done[g] = t_pv[k]

        def o_out(u):
            t_olo[u] = hi_lo(ps_o, oh[:, u % 3], ol[:, u % 3], t_pv[5 * u + 4], t_wod.get(u - 3), c_ohi, c_olo)

        def wo_pe(u, t):
            a, z, tt = 128 * t, 128 * t + 128, 4 * qg(u) + t
            pe.wait(t_olo[u], t_wo[head(u - 1)], t_wo[head(u)], m_free[0])
            terms = []
            for w in (u - 1, u):
                h = head(w)
                terms += split3(oh[:, w % 3, a:z], ol[:, w % 3, a:z], woh[:, h % 3], wol[:, h % 3])
            tok = products(ps_m, terms, c_wo)
            for w in (u - 1, u):
                t_wod[w] = tok
                wo_done[head(w)] = tok
            t_wop[tt] = tok

        def wo_add(u, t):
            tt = 4 * qg(u) + t
            dve.wait(t_wop[tt], t_addx[tt])
            m_free[0] = t_addx[tt] = dve.do(lambda e: e.tensor_tensor(
                xacc[:, tt, :], ps_m, xacc[:, tt, :], ALU.add), c_add)

        def wo_steps(u):
            w, half = (u - 1, 0) if u % 2 == 0 else (u - 2, 1)
            return [(w, 2 * half), (w, 2 * half + 1)] if 1 <= w < UNITS else []

        def real(u):
            return 0 <= u < UNITS

        prefetch(1)
        q_pe(0, 0)
        q_pe(0, 1)
        q_out(0)
        q_pe(1, 0)
        q_pe(1, 1)
        for u in range(-1, UNITS + 2):
            nxt_, cur, todo = real(u + 1), real(u), wo_steps(u)
            prefetch(u + 2)

            def new(fn, t):
                if nxt_:
                    fn(u + 1, t)

            def old(fn, j):
                if cur:
                    fn(u, j)

            def wo_do(fn, i):
                if todo:
                    fn(*todo[i])

            new(s_pe, 0)
            if real(u + 2):
                q_out(u + 2)
            old(tr_hi, 1)
            new(s_max, 0)
            old(tr_lo, 1)
            new(s_exp, 0)
            old(pv_pe, 0)
            wo_do(wo_pe, 0)
            new(s_norm, 0)
            old(tr_pe, 2)
            wo_do(wo_add, 0)
            new(s_pe, 1)
            old(tr_hi, 2)
            new(s_max, 1)
            old(tr_lo, 2)
            new(s_exp, 1)
            old(pv_pe, 1)
            old(tr_pe, 3)
            wo_do(wo_pe, 1)
            new(s_norm, 1)
            old(tr_hi, 3)
            old(tr_lo, 3)
            new(s_pe, 2)
            wo_do(wo_add, 1)
            new(s_max, 2)
            new(s_exp, 2)
            old(pv_pe, 2)
            old(tr_pe, 4)
            new(s_norm, 2)
            old(tr_hi, 4)
            new(s_pe, 3)
            new(s_max, 3)
            old(tr_lo, 4)
            new(s_exp, 3)
            old(pv_pe, 3)
            new(s_norm, 3)
            for kind, n in plan.get(u, []):
                run_task(kind, n, pending.pop((kind, n)))
            old(pv_pe, 4)
            if real(u + 3):
                q_pe(u + 3, 0)
            if cur:
                o_out(u)
            new(tr_pe, 0)
            new(tr_hi, 0)
            new(tr_lo, 0)
            if real(u + 3):
                q_pe(u + 3, 1)
            new(tr_pe, 1)

        def barrier():
            toks = [(c, c.n) for c in counts if c.n]
            for e in (pe, dve, act, pool, sp):
                e.wait(toks)

        counts = ([c_init, c_cst, c_xtr, c_xhi, c_xlo, c_gk, c_gv, c_wtr, c_whi, c_wlo, c_kv, c_kvd, c_kva, c_kvp, c_vn,
                   c_q, c_qhi, c_qlo, c_s, c_max, c_exp, c_rec, c_p, c_tr, c_phi, c_plo, c_pv, c_ohi, c_olo,
                   c_wo, c_add, c_ln, c_lna, c_bo, c_sub, c_sub2, c_sum, c_ff, c_ffa, c_ffd] + c_raw + c_x)
        barrier()
        one.close()

        two = ExitStack()
        HT = NT // 2
        x2h, x2l = pair("x2T", [128, NC, 1024], two)
        cth, ctl = pair("ctT", [128, NC, 1024], two)
        wqh2, wql2 = pair("xwq", [128, 4, 512], two)
        wkh2, wkl2 = pair("xwk", [128, 2, 512], two)
        wvh2, wvl2 = pair("xwv", [128, NC, 2, 128], two)
        uh, ul = pair("xwo", [128, 4, 512], two)
        raw2 = sb("raw2", [128, 4, 512], F32, two)
        k2 = sb("xk", [128, 16, 2, 64], F32R, two)
        v2h, v2l = pair("xv", [128, HT, 256], two)
        q2h, q2l = pair("xq", [128, 4, 2, 128], two)
        sB = sb("sB", [128, 2, 256], F32, two)
        P2 = sb("P2", [128, 2, 256], F32, two)
        p2h, p2l = pair("xp", [128, 512], two)
        o2h, o2l = pair("xo", [128, 8, 128], two)
        bob = sb("bob", [128, 512], F32, two)
        bsrc = sb("bsrc", [48, 128], F32, two)
        mx2 = sb("mx2", [128, 8], F32, two)
        sm2 = sb("sm2", [128, 8], F32, two)

        ps_q = [big[0][:, 0, :], big[0][:, 1, :]]
        ps_sc = big[1]
        ps_ov = [big[2][:, 0, :], big[2][:, 1, :]]
        ps_tp = bank[0][:, :]
        ps_w = bank[1][:, :]

        raw2_free = [None] * 4
        raw2_n = [0]

        def load2(src, blocks):
            s = raw2_n[0] % 4
            raw2_n[0] += 1
            sp.wait(raw2_free[s])
            dst = raw2[:, s, :].rearrange("p (o d) -> p o d", d=128) if blocks else raw2[:, s, :]
            return s, sp.do(lambda e: e.dma_start(dst, src), c_raw[s], 16)

        wq2_v = xWq.rearrange("(c p) (h d) -> h p c d", p=128, d=128)
        wkv2_v = xWkv.rearrange("(c p) (h d) -> h p c d", p=128, d=128)
        wo2_v = xWo.rearrange("(h p) n -> h p n", p=128)

        GG = 2 * G
        STEPS = 4 * GG

        def blocks_at(g, s):
            if s == 2:
                return [("wq", 4 * (g + 1) + j) for j in range(4)] if g + 1 < GG else []
            if s == 0:
                return [("wo", 4 * g + j) for j in range(4)]
            if s == 1:
                a = [("wk", g + 2)] if g + 2 < GG else []
                return a + ([("wv", g + 2), ("wv", g + 3)] if g % 2 == 0 and g + 2 < GG else [])
            return []

        def tiles_at(g, s):
            return [HT + 2 * s, HT + 2 * s + 1] if g == G - 1 else []

        first = [("wk", 0), ("ctx", 0), ("ctx", 1), ("wv", 0), ("wv", 1)] + [("wq", j) for j in range(4)]
        for t in range(2, HT):
            first.append(("ctx", t))
        first.append(("wk", 1))
        line = list(first)
        for n in range(STEPS):
            line += [("ctx", t) for t in tiles_at(n // 4, n % 4)] + blocks_at(n // 4, n % 4)
        fetched = {}
        at = [0, 0]

        def source(kind, n):
            if kind == "wq":
                return wq2_v[n % NH], True
            if kind == "wk":
                return wkv2_v[n % G], True
            if kind == "wv":
                return wkv2_v[G + n % G], True
            if kind == "wo":
                return wo2_v[n % NH], False
            return cf[128 * n:128 * n + 128, :], False

        def take(kind, n):
            assert line[at[1]] == (kind, n), (line[at[1]], kind, n)
            while at[0] < min(len(line), at[1] + 4):
                fetched[line[at[0]]] = load2(*source(*line[at[0]]))
                at[0] += 1
            at[1] += 1
            return fetched.pop((kind, n))

        t_w, w_done = {}, {}

        def weight2(kind, n):
            s, t_in = take(kind, n)
            blk = raw2[:, s, :]
            if kind == "wq":
                hi, lo, old = wqh2[:, n % 4], wql2[:, n % 4], n - 4
            elif kind == "wo":
                hi, lo, old = uh[:, n % 4], ul[:, n % 4], n - 4
            elif kind == "wk":
                hi, lo, old = wkh2[:, n % 2], wkl2[:, n % 2], n - 2
            else:
                hi, lo, old = wvh2[:, :, n % 2, :], wvl2[:, :, n % 2, :], n - 2
                blk = blk.rearrange("p (c d) -> p c d", d=128)
            act.wait(t_in, w_done.get((kind, old)))
            a = act.do(lambda e: e.activation(hi, blk, ACT.Copy), c_whi)
            pool.wait(a)
            t_w[(kind, n)] = raw2_free[s] = pool.do(lambda e: e.tensor_tensor(lo, blk, f(hi), ALU.subtract), c_wlo)

        q_free, q_turn = [None, None], [0]

        def q_bank():
            b = q_turn[0] % 2
            q_turn[0] += 1
            pe.wait(q_free[b])
            return b, ps_q[b]

        t_x2, t_ct = [None] * NT, [None] * NT
        x2_done, ct_done = [None] * 4, [None] * 4

        def tile2(srcs, t_in, hT, lT, col, t_free):
            b, ps = q_bank()
            pe.wait(t_in, t_id)
            t = transposes(ps, srcs, c_xtr)
            q_free[b] = hi_lo(ps.rearrange("p (c t) -> p c t", c=NC), hT[:, :, col:col + 128],
                              lT[:, :, col:col + 128], t, t_free, c_xhi, c_xlo)
            return t, q_free[b]

        def ctx_tile(tt):
            s, t_in = take("ctx", tt)
            i = tt % HT
            raw2_free[s], t_ct[tt] = tile2([raw2[:, s, 128 * c:128 * c + 128] for c in range(NC)], t_in,
                                           cth, ctl, 128 * i, ct_done[i // 2])

        def x2_tile(tt, t_in):
            i = tt % HT
            t, t_x2[tt] = tile2([xacc[:, tt, 128 * c:128 * c + 128] for c in range(NC)], t_in,
                                x2h, x2l, 128 * i, x2_done[i // 2])
            pool.wait(t, t_b)
            t_addx[tt] = pool.do(lambda e: e.tensor_tensor(xacc[:, tt, :], xacc[:, tt, :], bob[:, :], ALU.add), c_bo)

        def rows2(g, s):
            return [HT * (g // G) + 2 * s, HT * (g // G) + 2 * s + 1]

        t_q2, t_k2, t_v2, t_s2, t_p2, t_pt2, t_pv2, t_o2 = {}, {}, {}, {}, {}, {}, {}, {}
        t_wo2, t_tr2 = {}, {}
        w_free = [None]

        def qproj(n, p):
            g, s = n // 4, n % 4
            c0 = 256 * s
            b, ps = q_bank()
            pe.wait([t_x2[t] for t in rows2(g, s)])
            for j in range(2):
                h = 4 * g + 2 * p + j
                pe.wait(t_w[("wq", h)])
                terms = []
                for c in range(NC):
                    w = slice(128 * c, 128 * c + 128)
                    terms += split3(wqh2[:, h % 4, w], wql2[:, h % 4, w], x2h[:, c, c0:c0 + 256], x2l[:, c, c0:c0 + 256])
                t = products(ps[:, 256 * j:256 * j + 256], terms, c_q)
                w_done[("wq", h)] = t
            x2_done[s] = t
            views = []
            act.wait(t, t_s2.get(n - 1), t_bqk)
            for j in range(2):
                h = (4 * g + 2 * p + j) % NH
                hi, lo = q2h[:, :, p, 64 * j:64 * j + 64], q2l[:, :, p, 64 * j:64 * j + 64]
                src = ps[:, 256 * j:256 * j + 256].rearrange("p (b i) -> p b i", i=64)
                views.append((hi, lo, src, bqk[:, h:h + 1]))
                a = act.do(lambda e, hi=hi, src=src, h=h: e.activation(
                    hi, src, ACT.Identity, bias=bqk[:, h:h + 1]), c_qhi)
            dve.wait(a)
            for hi, lo, src, bq in views:
                t = dve.do(lambda e, hi=hi, lo=lo, src=src, bq=bq: e.scalar_tensor_tensor(
                    lo, src, bq, f(hi), ALU.add, ALU.subtract), c_qlo)
            q_free[b] = t_q2[n] = t

        def kproj(g, s):
            c0 = 256 * s
            b, ps = q_bank()
            pe.wait(t_w[("wk", g)], [t_ct[t] for t in rows2(g, s)])
            terms = []
            for c in range(NC):
                w = slice(128 * c, 128 * c + 128)
                terms += split3(wkh2[:, g % 2, w], wkl2[:, g % 2, w], cth[:, c, c0:c0 + 256], ctl[:, c, c0:c0 + 256])
            t = products(ps[:, 0:256], terms, c_kv)
            w_done[("wk", g)] = t
            ct_done[s] = t
            src = ps[:, 0:256].rearrange("p (b i) -> p b i", i=64)
            hi, lo = k2[:, 4 * s:4 * s + 4, 0, :], k2[:, 4 * s:4 * s + 4, 1, :]
            bk = bqk[:, 32 + g % G:33 + g % G]
            act.wait(t, t_s2.get(4 * (g - 1) + s), t_bqk)
            a = act.do(lambda e: e.activation(hi, src, ACT.Identity, bias=bk), c_kva)
            dve.wait(a)
            q_free[b] = t_k2[(g, s)] = dve.do(lambda e: e.scalar_tensor_tensor(
                lo, src, bk, f(hi), ALU.add, ALU.subtract), c_kvd)

        def vproj(g, s):
            b, ps = q_bank()
            pe.wait(t_w[("wv", g)], t_w[("wv", g + 1)], [t_ct[t] for t in rows2(g, s)])
            for i in range(2):
                a0 = 256 * s + 128 * i
                terms = []
                for c in range(NC):
                    terms += split3(cth[:, c, a0:a0 + 128], ctl[:, c, a0:a0 + 128], flat(wvh2[:, c]), flat(wvl2[:, c]))
                t = products(ps[:, 256 * i:256 * i + 256], terms, c_kv)
            w_done[("wv", g)] = w_done[("wv", g + 1)] = t
            ct_done[s] = t
            q_free[b] = t_v2[(g, s)] = t_v2[(g + 1, s)] = hi_lo(
                ps, flat(v2h[:, 2 * s:2 * s + 2, :]), flat(v2l[:, 2 * s:2 * s + 2, :]),
                t, t_pv2.get(4 * (g - 1) + s), c_kva, c_kvd)

        def scores2(n):
            g, s = n // 4, n % 4
            pe.wait(t_q2[n], t_k2[(g, s)], t_p2.get(("add", n - 1)))
            tok = []
            for bp in range(2):
                for p in range(2):
                    for bo in range(2):
                        i = 2 * bp + bo
                        kk = flat(k2[:, 4 * s + i])
                        c0 = 256 * p + 128 * bo
                        t = products(ps_sc[:, bp, c0:c0 + 128], [(q2h[:, i, p], kk), (q2l[:, i, p], kk)], c_s)
                tok.append(t)
            t_s2[n] = t
            for bp in range(2):
                ab = ps_sc[:, bp, :].rearrange("p (x a k) -> p x a k", a=2, k=64)
                low = sB[:, bp].rearrange("p (x k) -> p x k", k=64)
                dst = P2[:, bp].rearrange("p (x k) -> p x k", k=64)
                act.wait(tok[bp], t_p2.get(("add", n - 1)))
                a = act.do(lambda e, low=low, ab=ab: e.activation(low, ab[:, :, 1, :], ACT.Copy), c_sub)
                dve.wait(a, t_tr2.get(n - 1))
                d = dve.do(lambda e, low=low, ab=ab, dst=dst: e.tensor_tensor(dst, ab[:, :, 0, :], low, ALU.add), c_sub2)
            t_p2[("add", n)] = d
            pv = flat(P2[:, :, :]).rearrange("p (x k) -> p x k", k=64)
            dve.wait(d)
            m = dve.do(lambda e: e.tensor_reduce(mx2[:, :], pv, AX.X, ALU.max), c_max)
            dve.wait(m)
            d = dve.do(lambda e: e.tensor_tensor(
                pv, pv, mx2[:, :].unsqueeze(2).to_broadcast([128, 8, 64]), ALU.subtract), c_max)
            act.wait(d)
            t_p2[("exp", n)] = act.do(lambda e: e.activation(
                flat(P2[:, :, :]), flat(P2[:, :, :]), ACT.Exp, scale=SCALE), c_exp)

        def softmax2(n):
            pv = flat(P2[:, :, :]).rearrange("p (x k) -> p x k", k=64)
            dve.wait(t_p2[("exp", n)])
            a = dve.do(lambda e: e.tensor_reduce(sm2[:, :], pv, AX.X, ALU.add), c_sum)
            dve.wait(a)
            a = dve.do(lambda e: e.reciprocal(sm2[:, :], sm2[:, :]), c_rec)
            pool.wait(a)
            t_p2[n] = pool.do(lambda e: e.tensor_tensor(
                pv, pv, sm2[:, :].unsqueeze(2).to_broadcast([128, 8, 64]), ALU.mult), c_p)

        def turn2(n):
            pe.wait(t_p2[n], t_pt2.get(n - 1))
            t_tr2[n] = transposes(ps_tp, [flat(P2[:, :, :])[:, 128 * b:128 * b + 128] for b in range(4)], c_tr)
            t_pt2[n] = hi_lo(ps_tp, p2h[:, :], p2l[:, :], t_tr2[n], t_pv2.get(n - 1), c_phi, c_plo)

        def values2(n):
            g, s = n // 4, n % 4
            pe.wait(t_pt2[n], t_v2[(g, s)], t_o2.get(n - 1))
            for bp in range(2):
                for par in range(2):
                    r = slice(64 * par, 64 * par + 64)
                    cc = slice(256 * bp, 256 * bp + 256)
                    d = slice(128 * (g % 2), 128 * (g % 2) + 128)
                    t = products(ps_ov[par][:, cc], split3(v2h[r, 2 * s + bp, d], v2l[r, 2 * s + bp, d],
                                                           p2h[r, cc], p2l[r, cc]), c_pv)
            t_pv2[n] = t
            bv = bqk[:, 40 + g % G:41 + g % G]
            act.wait(t, t_wo2.get(n - 1), t_bqk)
            for par in range(2):
                src = ps_ov[par].rearrange("p (x i) -> p x i", i=64)
                hi, lo = o2h[:, :, 64 * par:64 * par + 64], o2l[:, :, 64 * par:64 * par + 64]
                a = act.do(lambda e, hi=hi, src=src: e.activation(hi, src, ACT.Identity, bias=bv), c_ohi)
                dve.wait(a)
                t_o2[n] = dve.do(lambda e, hi=hi, lo=lo, src=src: e.scalar_tensor_tensor(
                    lo, src, bv, f(hi), ALU.add, ALU.subtract), c_olo)

        def wo2(n, i):
            if n < 0:
                return
            g, s = n // 4, n % 4
            tt = rows2(g, s)[i]
            pe.wait(t_o2[n], w_free[0])
            for j in range(4):
                pe.wait(t_w[("wo", 4 * g + j)])
                t = products(ps_w, split3(o2h[:, 4 * i + j], o2l[:, 4 * i + j], uh[:, j], ul[:, j]),
                             c_wo if j == 3 else None, first=j == 0, final=j == 3)
            for j in range(4):
                w_done[("wo", 4 * g + j)] = t
            t_wo2[n] = t
            dve.wait(t, t_addx[tt])
            w_free[0] = t_addx[tt] = dve.do(lambda e: e.tensor_tensor(
                xacc[:, tt, :], ps_w, xacc[:, tt, :], ALU.add), c_add)

        sp.do(lambda e: e.dma_start(bob[:, :], xbo.rearrange("(a d) -> a d", a=1).to_broadcast([128, 512])), c_cst, 16)
        sp.do(lambda e: e.dma_start(bsrc[0:32, :], xbq.rearrange("(h d) -> h d", d=128)), c_cst, 16)
        t_b = sp.do(lambda e: e.dma_start(bsrc[32:48, :], xbkv.rearrange("(h d) -> h d", d=128)), c_cst, 16)
        t_ln = [None] * 4

        def ln2(q):
            ts = list(range(4 * q, 4 * q + 4))
            t_ln[q] = layernorm(ts, [t_addx[t] for t in ts])

        weight2("wk", 0)
        pe.wait(t_b)
        t = pe.do(lambda e: e.transpose(ps_w[:, 0:48], bsrc[0:48, :], ident[0:48, 0:48]), c_xtr)
        dve.wait(t)
        t_bqk = dve.do(lambda e: e.tensor_copy(bqk[:, :], ps_w[:, 0:48]), c_kvd)
        w_free[0] = t_bqk
        ctx_tile(0)
        ctx_tile(1)
        ln2(0)
        kproj(0, 0)
        weight2("wv", 0)
        weight2("wv", 1)
        x2_tile(0, t_ln[0])
        x2_tile(1, t_ln[0])
        for j in range(4):
            weight2("wq", j)
        vproj(0, 0)
        ln2(1)
        qproj(0, 0)
        qproj(0, 1)
        for s in range(1, 4):
            for tt in rows2(0, s):
                ctx_tile(tt)
            for tt in rows2(0, s):
                x2_tile(tt, t_ln[tt // 4])
            kproj(0, s)
            vproj(0, s)
        weight2("wk", 1)

        for n in range(STEPS):
            g, s = n // 4, n % 4
            work = blocks_at(g, s)
            scores2(n)
            wo2(n - 1, 0)
            softmax2(n)
            if n + 1 < STEPS:
                qproj(n + 1, 0)
                qproj(n + 1, 1)
            turn2(n)
            wo2(n - 1, 1)
            fresh = tiles_at(g, s)
            for tt in fresh:
                ctx_tile(tt)
            for a in work[:2]:
                weight2(*a)
            values2(n)
            for tt in fresh:
                x2_tile(tt, t_ln[tt // 4])
            if g + 1 < GG:
                kproj(g + 1, s)
                if g % 2 == 1:
                    vproj(g + 1, s)
            for a in work[2:]:
                weight2(*a)
            if n in (1, 3):
                ln2(2 + n // 2)
        wo2(STEPS - 1, 0)
        wo2(STEPS - 1, 1)
        barrier()
        two.close()

        three = ExitStack()
        x3h, x3l = pair("x3T", [128, NC, T], three)
        fwh, fwl = pair("fwT", [128, NC, D], three)
        fah, fal = pair("fa", [128, NC, E_R], three)
        fbh, fbl = pair("fbm", [128, D], three)
        raw3 = sb("raw3", [128, 4, 512], F32, three)
        rawa = sb("rawa", [128, 4, 128], F32, three)
        rawb = sb("rawb", [128, 512], F32, three)
        fbb = sb("fbb", [128, 512], F32, three)
        uTh, uTl = pair("uT", [128, 512], three)
        z = sb("z", [128, 2, 512], F32, three)
        junk = sb("junk", [128, 512], F32, three)
        nrm = sb("nrm", [128, 4, 2], F32, three)
        nz = sb("nz", [128, 4, 2], F32, three)
        gam = sb("gam", [128, 4], F32, three)

        sp.do(lambda e: e.dma_start(raw3[:, :, :], fW.rearrange("(o p) d -> p o d", p=128)), c_cst, 16)
        sp.do(lambda e: e.dma_start(fbb[:, :], fb.rearrange("(a d) -> a d", a=1).to_broadcast([128, 512])), c_cst, 16)
        for c in range(NC):
            sp.do(lambda e, c=c: e.dma_start(
                rawa[:, c, :].rearrange("p (x r) -> p x r", r=16),
                fA[:, 128 * c:128 * c + 128, :].rearrange("x p r -> p x r")), c_cst, 16)
        sp.do(lambda e: e.dma_start(rawb[:, :], fB.rearrange("x r o -> (x r) o")), c_cst, 16)
        t_f = sp.do(lambda e: e.dma_start(
            pcol[:, :], fp.rearrange("(x o) -> x o", o=1).unsqueeze(1).to_broadcast([8, 16, 1]),
            allow_slow_non_contiguous=True), c_cst, 16)

        xbanks3 = [bank[0][:, :], bank[1][:, :]]
        for k in list(turn):
            if isinstance(k, tuple):
                turn.pop(k)
        turn["x"] = 0
        for o in range(4):
            _, t_fw = transposed_tile(o, [raw3[:, o, 128 * c:128 * c + 128] for c in range(NC)], t_f,
                                      fwh, fwl, 128 * o, xbanks3)
        act.wait(t_f)
        a = act.do(lambda e: e.activation(flat(fah[:, :, :]), flat(rawa[:, :, :]), ACT.Copy), c_ffa)
        dve.wait(a)
        dve.do(lambda e: e.tensor_tensor(flat(fal[:, :, :]), flat(rawa[:, :, :]), f(flat(fah[:, :, :])), ALU.subtract),
               c_ffd)
        a = act.do(lambda e: e.activation(fbh[:, :], rawb[:, :], ACT.Copy), c_ffa)
        dve.wait(a)
        t_fab = dve.do(lambda e: e.tensor_tensor(fbl[:, :], rawb[:, :], f(fbh[:, :]), ALU.subtract), c_ffd)

        t_ln3 = [layernorm(list(range(4 * q, 4 * q + 4)), [t_addx[t] for t in range(4 * q, 4 * q + 4)])
                 for q in range(4)]
        t_x3 = [None] * NT
        for tt in range(NT):
            _, t_x3[tt] = transposed_tile(tt, [xacc[:, tt, 128 * c:128 * c + 128] for c in range(NC)],
                                          t_ln3[tt // 4], x3h, x3l, 128 * tt, xbanks3)
        ps_u = big[0][:, 0, :]
        ps_z = [big[1][:, 0, :], big[1][:, 1, :]]
        ps_mm = [big[2][:, 0, :], big[2][:, 1, :]]
        z_free, mm_free, u_free, uslot = [None, None], [None, None], None, None
        t_zs = [None, None]
        gam_free = [None] * 4
        t_n = None
        for q in range(4):
            c0 = 512 * q
            pe.wait([t_x3[t] for t in range(4 * q, 4 * q + 4)], t_fab, t_fw, u_free)
            terms = []
            for c in range(NC):
                terms += split3(fah[:, c, :], fal[:, c, :], x3h[:, c, c0:c0 + 512], x3l[:, c, c0:c0 + 512])
            t = products(ps_u, terms, c_ff)
            act.wait(t, uslot)
            a = act.do(lambda e: e.activation(uTh[:, :], ps_u, ACT.Identity, scale=pcol[:, 0:1]), c_ffa)
            dve.wait(a)
            u_free = dve.do(lambda e: e.scalar_tensor_tensor(
                uTl[:, :], ps_u, pcol[:, 0:1], f(uTh[:, :]), ALU.mult, ALU.subtract), c_ffd)
            for i in range(4):
                tt = 4 * q + i
                b = tt % 2
                s = slice(128 * tt, 128 * tt + 128)
                us = slice(128 * i, 128 * i + 128)
                pe.wait(z_free[b])
                terms = []
                for c in range(NC):
                    terms += split3(x3h[:, c, s], x3l[:, c, s], fwh[:, c, :], fwl[:, c, :])
                t_z = products(ps_z[b], terms, c_ff)
                pe.wait(u_free, mm_free[b])
                t_m = products(ps_mm[b], split3(uTh[:, us], uTl[:, us], fbh[:, :], fbl[:, :]), c_ff)
                uslot = t_m
                dve.wait(t_z, t_zs[b])
                z_free[b] = t_zz = dve.do(lambda e, b=b: e.tensor_tensor(z[:, b, :], ps_z[b], fbb[:, :], ALU.add),
                                          c_ffd)
                act.wait(t_zz, t_n)
                a = act.do(lambda e, b=b, i=i: e.activation(junk[:, :], z[:, b, :], ACT.Square,
                                                            accum_out=nrm[:, i, 0:1]), c_ffa)
                act.wait(t_m, a)
                a = act.do(lambda e, b=b, i=i: e.activation(junk[:, :], ps_mm[b], ACT.Square,
                                                            accum_out=nrm[:, i, 1:2]), c_ffa)
                act.wait(a)
                a = act.do(lambda e, i=i: e.activation(nz[:, i, :], nrm[:, i, :], ACT.Sqrt), c_ffa)
                t_n = a
                dve.wait(a)
                d = dve.do(lambda e, i=i: e.tensor_scalar(nz[:, i, 1:2], nz[:, i, 1:2], 1e-6, None, ALU.add), c_ffd)
                dve.wait(d)
                d = dve.do(lambda e, i=i: e.reciprocal(nz[:, i, 1:2], nz[:, i, 1:2]), c_ffd)
                dve.wait(d)
                d = dve.do(lambda e, i=i: e.scalar_tensor_tensor(
                    gam[:, i:i + 1], nz[:, i, 0:1], 0.5, nz[:, i, 1:2], ALU.mult, ALU.mult), c_ffd)
                dve.wait(d)
                d = dve.do(lambda e, i=i: e.tensor_scalar(gam[:, i:i + 1], gam[:, i:i + 1], 1.0, None, ALU.min), c_ffd)
                dve.wait(d)
                d = dve.do(lambda e, b=b, i=i: e.scalar_tensor_tensor(
                    z[:, b, :], ps_mm[b], gam[:, i:i + 1], z[:, b, :], ALU.mult, ALU.add), c_ffd)
                mm_free[b] = d
                dve.wait(d, t_x3[tt])
                t_zs[b] = t_addx[tt] = dve.do(lambda e, b=b, tt=tt: e.tensor_tensor(
                    xacc[:, tt, :], xacc[:, tt, :], z[:, b, :], ALU.add), c_add)
            t_l = layernorm(list(range(4 * q, 4 * q + 4)), [t_addx[4 * q + 3]])
            sp.wait(t_l)
            t_out = sp.do(lambda e, c0=c0, q=q: e.dma_start(
                of[c0:c0 + 512, :].rearrange("(t p) d -> p t d", p=128), xacc[:, 4 * q:4 * q + 4, :]), c_out, 16)
        sp.wait(t_out)
        three.close()

        block = top.enter_context(nc.Block())

        @block.sync
        def _(e):
            sp.run(e)

        @block.gpsimd
        def _(e):
            pool.run(e)

        @block.scalar
        def _(e):
            act.run(e)

        @block.vector
        def _(e):
            dve.run(e)

        @block.tensor
        def _(e):
            pe.run(e)


_INS = ['x', 'ctx_4096', 'L0_attn_freqs_cos', 'L0_attn_freqs_sin', 'L0_attn_wq', 'L0_attn_wk', 'L0_attn_wv',
        'L0_attn_wo', 'L0_attn_k_cache', 'L0_attn_v_cache', 'L0_attn_block_idx', 'L0_xattn_Wq', 'L0_xattn_bq',
        'L0_xattn_Wkv', 'L0_xattn_bkv', 'L0_xattn_Wo', 'L0_xattn_bo', 'L0_ffn_W', 'L0_ffn_b', 'L0_ffn_A',
        'L0_ffn_B', 'L0_ffn_p_scores']


def kernel(**inputs):
    import numpy as np
    import concourse.bacc as bacc
    from concourse.bass_utils import run_bass_kernel_spmd as run

    nc = bacc.Bacc("TRN2", target_bir_lowering=False, num_devices=1)
    arrays, args = {}, []
    for name in _INS:
        a = np.ascontiguousarray(inputs[name])
        arrays[f"in_{name}"] = a
        args.append(nc.dram_tensor(f"in_{name}", a.shape, mybir.dt.from_np(a.dtype), kind="ExternalInput").ap())
    o = nc.dram_tensor("out_0", (32, 64, 512), F32, kind="ExternalOutput").ap()
    decoder_kernel(nc, *args, o)
    r = run(nc, [arrays], core_ids=[0])
    return r.results[0]["out_0"]
```

```python
import concourse.bass as bass
from concourse import mybir
from contextlib import ExitStack

F32 = mybir.dt.float32
F32R = mybir.dt.float32r
I32 = mybir.dt.int32
U32 = mybir.dt.uint32
ALU = mybir.AluOpType
ACT = mybir.ActivationFunctionType
AX = mybir.AxisListType

D = 512
T = 2048
NT = T // 128
NC = D // 128
NH = 32
G = 8
HD = 128
KEYS = 576
HALF = KEYS // 2
SCALE = float(HD) ** -0.5
LN_EPS = 1e-5
E_R = 128


class Count:

    def __init__(self, h):
        self.h, self.n = h, 0


class Queue:

    def __init__(self):
        self.ops, self.seen = [], {}

    def wait(self, *tokens):
        for t in tokens:
            if t is None:
                continue
            if isinstance(t, list):
                self.wait(*t)
                continue
            c, v = t
            if self.seen.get(id(c), 0) < v:
                self.seen[id(c)] = v
                self.ops.append(lambda e, h=c.h, v=v: e.wait_ge(h, v))

    def do(self, fn, count=None, by=1):
        if count is None:
            self.ops.append(fn)
            return None
        self.ops.append(lambda e: fn(e).then_inc(count.h, by))
        count.n += by
        return (count, count.n)

    def run(self, e):
        for op in self.ops:
            op(e)


def decoder_kernel(nc, x, ctx_in, fcos, fsin, wq, wk, wv, wo, k_cache, v_cache, block_idx,
                   xWq, xbq, xWkv, xbkv, xWo, xbo, fW, fb, fA, fB, fp, out):
    with ExitStack() as top:
        pe, dve, act, pool, sp = Queue(), Queue(), Queue(), Queue(), Queue()

        def sem(name):
            return Count(top.enter_context(nc.semaphore(name)))

        def sb(name, shape, dt=F32, scope=top):
            return scope.enter_context(nc.sbuf_tensor(name, shape, dt))

        def pair(name, shape, scope=top):
            return sb(name + "h", shape, F32R, scope), sb(name + "l", shape, F32R, scope)

        def f(ap):
            return ap.bitcast(F32)

        xf = x.rearrange("a b d -> (a b) d")
        cf = ctx_in.rearrange("a b d -> (a b) d")
        of = out.rearrange("a b d -> (a b) d")

        bank = [top.enter_context(nc.psum_tensor(f"bank{i}", [128, 512], F32)) for i in range(2)]
        big = [top.enter_context(nc.psum_tensor(f"big{i}", [128, 2, 512], F32)) for i in range(3)]
        ps_pt = [bank[0], bank[1]]
        ps_s = [big[0], big[1]]
        ps_o = big[2][:, 0, :]
        ps_m = big[2][:, 1, :]

        c_init = sem("c_init")
        c_x = [sem(f"c_x{i}") for i in range(7)]
        c_cst = sem("c_cst")
        c_idx = sem("c_idx")
        c_bob = sem("c_bob")
        c_pcol = sem("c_pcol")
        c_fbb = sem("c_fbb")
        c_xtr = sem("c_xtr")
        c_xhi = sem("c_xhi")
        c_xlo = sem("c_xlo")
        c_raw = [sem(f"c_raw{i}") for i in range(6)]
        c_gk = sem("c_gk")
        c_gv = sem("c_gv")
        c_wtr = sem("c_wtr")
        c_whi = sem("c_whi")
        c_wlo = sem("c_wlo")
        c_wlp = sem("c_wlp")
        c_kv = sem("c_kv")
        c_kvd = sem("c_kvd")
        c_kva = sem("c_kva")
        c_kvp = sem("c_kvp")
        c_vn = sem("c_vn")
        c_q = sem("c_q")
        c_qhi = sem("c_qhi")
        c_qlo = sem("c_qlo")
        c_s = sem("c_s")
        c_max = sem("c_max")
        c_exp = sem("c_exp")
        c_rec = sem("c_rec")
        c_dup = sem("c_dup")
        c_p = sem("c_p")
        c_tr = sem("c_tr")
        c_phi = sem("c_phi")
        c_plo = sem("c_plo")
        c_pv = sem("c_pv")
        c_ohi = sem("c_ohi")
        c_olo = sem("c_olo")
        c_wo = sem("c_wo")
        c_add = sem("c_add")
        c_ln = sem("c_ln")
        c_lna = sem("c_lna")
        c_bo = sem("c_bo")
        c_sub = sem("c_sub")
        c_sub2 = sem("c_sub2")
        c_sum = sem("c_sum")
        c_ff = sem("c_ff")
        c_ffa = sem("c_ffa")
        c_ffd = sem("c_ffd")
        c_out = sem("c_out")

        ident = sb("ident", [128, 128])
        xacc = sb("xacc", [128, NT, D])
        stat = sb("stat", [128, NT, 6])
        mv = sb("mv", [128, NT, 2])
        rstd = sb("rstd", [128, NT])
        bqk = sb("bqk", [128, 48])
        pcol = sb("pcol", [128, 1])
        xTh, xTl = pair("xT", [128, NC, T])
        wqh, wql = pair("wqT", [128, 4, NC, 128])
        wkvh, wkvl = pair("wkvT", [128, NC, 128])
        raw = sb("raw", [128, 3, 512])

        t_id0 = pool.do(lambda e: e.memset(ident[:, :], 0.0), c_init)
        pool.wait(t_id0)
        t_id = pool.do(lambda e: e.affine_select(
            out=ident[:, :], in_=ident[:, :], compare_op=ALU.not_equal, fill=1.0, base=0,
            pattern=[[-1, 128]], channel_multiplier=1), c_init)

        t_x = []

        def load_x(q):
            w = 1 if q == 0 else 4
            for a in range(4 * q, 4 * q + 4, w):
                t = sp.do(lambda e, a=a: e.dma_start(
                    xacc[:, a:a + w, :], xf[128 * a:128 * a + 128 * w, :].rearrange("(t p) d -> p t d", p=128)),
                    c_x[a if q == 0 else q + 3], 16)
                t_x.extend([t] * w)

        def products(dst, terms, count, first=True, final=True):
            tok = None
            for i, (a, b) in enumerate(terms):
                end = i == len(terms) - 1
                tok = pe.do(lambda e, a=a, b=b, s=first and i == 0, z=final and end:
                            e.matmul(dst, a, b, start=s, stop=z), count if end else None)
            return tok

        def split3(ah, al, bh, bl):
            return [(ah, bh), (ah, bl), (al, bh)]

        def transposes(dst, srcs, count):
            tok = None
            for i, s in enumerate(srcs):
                tok = pe.do(lambda e, i=i, s=s: e.transpose(dst[:, 128 * i:128 * i + 128], s, ident[:, :]),
                            count if i == len(srcs) - 1 else None)
            return tok

        def hi_lo(src, hi, lo, t_src, t_free, c_hi, c_lo):
            act.wait(t_src, t_free)
            a = act.do(lambda e: e.activation(hi, src, ACT.Copy), c_hi)
            dve.wait(a)
            return dve.do(lambda e: e.tensor_tensor(lo, src, f(hi), ALU.subtract), c_lo)

        t_stat = {}

        def ln_stats(tiles, t_in):
            a, b = tiles[0], tiles[-1] + 1
            dve.wait(t_in)
            for tt in tiles:
                t = dve.do(lambda e, tt=tt: e.bn_stats(stat[:, tt, :], xacc[:, tt, :]), c_ln)
            dve.wait(t)
            for tt in tiles:
                t = dve.do(lambda e, tt=tt: e.bn_aggr(mv[:, tt, :], stat[:, tt, :]), c_ln)
            dve.wait(t)
            t = dve.do(lambda e: e.tensor_scalar(mv[:, a:b, 1], mv[:, a:b, 1], LN_EPS, None, ALU.add), c_ln)
            for tt in tiles:
                t_stat[tt] = t

        t_rstd = {}

        def ln_root(tiles):
            a, b = tiles[0], tiles[-1] + 1
            act.wait([t_stat[t] for t in tiles])
            t = act.do(lambda e: e.activation(rstd[:, a:b], mv[:, a:b, 1], ACT.Sqrt), c_lna)
            for tt in tiles:
                t_rstd[tt] = t

        def ln_rows(tiles):
            a, b = tiles[0], tiles[-1] + 1
            dve.wait([t_rstd[t] for t in tiles])
            t = dve.do(lambda e: e.reciprocal(rstd[:, a:b], rstd[:, a:b]), c_ln)
            dve.wait(t)
            for tt in tiles:
                t = dve.do(lambda e, tt=tt: e.tensor_scalar(
                    xacc[:, tt, :], xacc[:, tt, :], mv[:, tt, 0:1], rstd[:, tt:tt + 1],
                    ALU.subtract, ALU.mult), c_ln)
            return t

        one = ExitStack()
        woh, wol = pair("woT", [128, 3, D], one)
        rkv = sb("rkv", [128, 4, 128], F32, one)
        krot = sb("krot", [128, 4, 128], F32, one)
        kTh, kTl = pair("kT", [128, 2, KEYS], one)
        vh, vl = pair("v", [128, 2, 4, 128], one)
        v4a, v4b = sb("v4a", [128, 2, 128], F32R, one), sb("v4b", [128, 2, 128], F32R, one)
        vtmp = sb("vtmp", [64, 128], F32R, one)
        P = sb("P", [128, 8, KEYS + 64], F32, one)
        pth, ptl = pair("pt", [128, 2, 512], one)
        qTh, qTl = pair("qT", [128, 2, 512], one)
        oh, ol = pair("oT", [128, 3, 512], one)
        cosb = sb("cosb", [128, 64], F32, one)
        sinb = sb("sinb", [128, 64], F32, one)
        ccol = sb("ccol", [128, 2], F32, one)
        cs2 = sb("cs2", [128, 1], F32, one)
        bidx = sb("bidx", [128, 4], I32, one)
        prow = sb("prow", [128, 1], I32, one)
        prowf = sb("prowf", [128, 1], F32, one)
        idx0 = sb("idx0", [128, 4], F32, one)
        idx = sb("idx", [128, G, 4], I32, one)
        nmx = sb("nmx", [128, 8], F32, one)
        rsum = sb("rsum", [128, 8], F32, one)
        rrec = sb("rrec", [128, 8], F32, one)

        bi = block_idx.rearrange("(k a) -> a k", a=4)
        for a in range(4):
            t_bi = sp.do(lambda e, a=a: e.dma_start(
                bidx[32 * a:32 * a + 32, :], bi[a:a + 1, :].to_broadcast([32, 4]), allow_slow_non_contiguous=True),
                c_idx, 16)
        load_x(0)

        def load_rotation():
            sp.do(lambda e: e.dma_start(cosb[:, :], fcos.to_broadcast([128, 64])), c_cst, 16)
            sp.do(lambda e: e.dma_start(sinb[:, :], fsin.to_broadcast([128, 64])), c_cst, 16)
            for i, v in enumerate((fcos, fsin)):
                t = sp.do(lambda e, i=i, v=v: e.dma_start(
                    ccol[:, i:i + 1], v.rearrange("a (d o) -> (a d) o", o=1).unsqueeze(1).to_broadcast([64, 2, 1]),
                    allow_slow_non_contiguous=True), c_cst, 16)
            return t

        t_row = t_id
        for a in range(4):
            pool.wait(t_row)
            t_row = pool.do(lambda e, a=a: e.iota(prow[32 * a:32 * a + 32, :], [[0, 1]], base=0,
                                                  channel_multiplier=8), c_init)
        def key_rows():
            dve.wait(t_bi, t_row)
            t = dve.do(lambda e: e.tensor_copy(prowf[:, :], prow[:, :]), c_kvd)
            dve.wait(t)
            t = dve.do(lambda e: e.tensor_scalar(idx0[:, :], bidx[:, :], 256.0, prowf[:, 0:1], ALU.mult, ALU.add), c_kvd)
            dve.wait(t)
            for g in range(G):
                t_idx = dve.do(lambda e, g=g: e.tensor_scalar(idx[:, g, :], idx0[:, :], float(g), None, ALU.add), c_kvd)
            return t_idx

        def rotation(t_c):
            dve.wait(t_c)
            t = dve.do(lambda e: e.tensor_scalar(cosb[:, :], cosb[:, :], SCALE, None, ALU.mult), c_kvd)
            t = dve.do(lambda e: e.tensor_scalar(sinb[:, :], sinb[:, :], SCALE, None, ALU.mult), c_kvd)
            t = dve.do(lambda e: e.tensor_tensor(ccol[:, :], ccol[:, :], ccol[:, :], ALU.mult), c_kvd)
            dve.wait(t)
            t = dve.do(lambda e: e.tensor_tensor(cs2[:, :], ccol[:, 0:1], ccol[:, 1:2], ALU.add), c_kvd)
            dve.wait(t)
            t_rot = dve.do(lambda e: e.tensor_scalar(cs2[:, :], cs2[:, :], SCALE, None, ALU.mult), c_kvd)
            return t_rot

        t_v4 = t_row
        for b in range(2):
            pool.wait(t_v4)
            t_v4 = pool.do(lambda e, b=b: e.memset(f(v4b[64:128, b, :]), 0.0), c_init)

        kc_v = k_cache.rearrange("n b h d -> (n b h) d")
        vc_v = v_cache.rearrange("n b h d -> (n b h) d")
        wq_v = wq.rearrange("(h p) d -> h p d", p=128)
        wk_v = wk.rearrange("(h p) d -> h p d", p=128)
        wv_v = wv.rearrange("(h p) d -> h p d", p=128)
        wo_v = wo.rearrange("(o p) (h d) -> h p o d", p=128, d=128)
        wq2_v = xWq.rearrange("(c p) (h d) -> h p c d", p=128, d=128)
        wkv2_v = xWkv.rearrange("(c p) (h d) -> h p c d", p=128, d=128)
        wo2_v = xWo.rearrange("(h p) n -> h p n", p=128)

        raws = [raw[:, s, :] for s in range(3)]
        raw_free = [None] * 6
        raw_n = [0]

        def raw_slot():
            s = raw_n[0] % len(raws)
            raw_n[0] += 1
            sp.wait(raw_free[s])
            return s

        def load_raw(dst_view, src):
            s = raw_slot()
            return s, sp.do(lambda e: e.dma_start(dst_view(raws[s]), src), c_raw[s], 16)

        def load_bias():
            s = raw_slot()
            sp.do(lambda e: e.dma_start(raws[s][0:32, 0:128], xbq.rearrange("(h d) -> h d", d=128)), c_raw[s], 16)
            return s, sp.do(lambda e: e.dma_start(raws[s][32:48, 0:128], xbkv.rearrange("(h d) -> h d", d=128)),
                            c_raw[s], 16)

        def as_rows(r):
            return r

        def as_blocks(r):
            return r.rearrange("p (o d) -> p o d", d=128)

        m_free = [None]
        pt_free, pt_n = [None, None], [0]

        def pt_bank():
            b = pt_n[0] % 2
            pt_n[0] += 1
            pe.wait(pt_free[b])
            return b, ps_pt[b][:, :]

        def weight(loaded, hi, lo, t_free):
            s, t_in = loaded
            b, ps = pt_bank()
            pe.wait(t_in, t_id)
            t = transposes(ps, [raws[s][:, 128 * c:128 * c + 128] for c in range(4)], c_wtr)
            raw_free[s] = t
            pt_free[b] = hi_lo(ps, hi, lo, t, t_free, c_whi, c_wlo)
            return pt_free[b]

        def split_weight(key, loaded, hi, lo, t_free, by_chunk=False, low=None):
            s, t_in = loaded
            blk = raws[s].rearrange("p (c d) -> p c d", d=128) if by_chunk else raws[s]
            act.wait(t_in, t_free)
            a = act.do(lambda e: e.activation(hi, blk, ACT.Copy), c_whi)
            eng, count = low or (pool, c_wlp)
            eng.wait(a)
            t_w[key] = raw_free[s] = eng.do(lambda e: e.tensor_tensor(lo, blk, f(hi), ALU.subtract), count)

        def token_tile(ps, t_bank_free, srcs, t_in, col, t_free):
            pe.wait(t_in, t_id, t_bank_free)
            t = transposes(ps, srcs, c_xtr)
            lo = hi_lo(ps.rearrange("p (c t) -> p c t", c=NC), xTh[:, :, col:col + 128],
                       xTl[:, :, col:col + 128], t, t_free, c_xhi, c_xlo)
            return t, lo

        CT = 1024
        t_w, w_done = {}, {}
        t_ct = [None] * NT
        t_wq, t_wo, t_kT, t_v, t_kn, t_vn = {}, {}, {}, {}, {}, {}
        wq_done, wo_done = {}, {}
        k_done, v_done = {}, {}
        t_xT = [None] * 4
        state = {}

        def flat(ap):
            return ap.rearrange("p c d -> p (c d)")

        def gather(g, what, dst, src, count, t_free):
            pool.wait(t_idx, t_free)
            for b in range(4):
                t = pool.do(lambda e, b=b: e.indirect_dma_start(
                    dst[:, b, :], None, src, bass.IndirectOffsetOnAxis(ap=idx[:, g, b:b + 1].bitcast(U32), axis=0)),
                    count, 16)
            state[what] = t

        def task(kind, n):
            if kind == "wq":
                return ("wq", n, lambda: load_raw(as_rows, wq_v[n]))
            if kind == "wo":
                return ("wo", n, lambda: load_raw(as_blocks, wo_v[n]))
            if kind == "wk":
                return ("wk", n, lambda: load_raw(as_rows, wk_v[n]))
            if kind == "wv":
                return ("wv", n, lambda: load_raw(as_rows, wv_v[n]))
            if kind == "xwq":
                return (kind, n, lambda: load_raw(as_blocks, wq2_v[n]))
            if kind == "xwk":
                return (kind, n, lambda: load_raw(as_blocks, wkv2_v[n]))
            if kind == "ctx":
                return (kind, n, lambda: load_raw(as_rows, cf[128 * n:128 * n + 128, :]))
            if kind == "bias":
                return (kind, n, load_bias)
            return (kind, n, lambda: None)

        def run_task(kind, n, loaded):
            if kind == "wq":
                t_wq[n] = weight(loaded, flat(wqh[:, n % 4]), flat(wql[:, n % 4]), wq_done.get(n - 4))
            elif kind == "wo":
                t_wo[n] = weight(loaded, woh[:, n % 3], wol[:, n % 3], wo_done.get(n - 3))
            elif kind in ("wk", "wv"):
                state[kind] = weight(loaded, flat(wkvh[:, :, :]), flat(wkvl[:, :, :]), state.get("wkv_done"))
            elif kind == "gk":
                gather(n, "gk", rkv, kc_v, c_gk, state.get("rkv_done"))
            elif kind == "gv":
                gather(n, "gv", rkv, vc_v, c_gv, state.get("rkv_done"))
            elif kind == "rot":
                b = n % 2
                dve.wait(state["gk"], t_rot, state.get("krot_done"))
                src = rkv[:, :, :].rearrange("p b (d o) -> p b d o", o=2)
                dst = krot[:, :, :].rearrange("p b (d o) -> p b d o", o=2)
                cb = cosb[:, :].unsqueeze(1).to_broadcast([128, 4, 64])
                sn = sinb[:, :].unsqueeze(1).to_broadcast([128, 4, 64])
                for o in range(2):
                    t = dve.do(lambda e, o=o: e.tensor_tensor(dst[:, :, :, o], src[:, :, :, o], cb, ALU.mult), c_kvd)
                dve.wait(t)
                for o in range(2):
                    t = dve.do(lambda e, o=o: e.tensor_tensor(src[:, :, :, o], src[:, :, :, o], sn, ALU.mult), c_kvd)
                dve.wait(t)
                dve.do(lambda e: e.tensor_tensor(dst[:, :, :, 0], dst[:, :, :, 0], src[:, :, :, 1], ALU.add), c_kvd)
                t = dve.do(lambda e: e.tensor_tensor(dst[:, :, :, 1], dst[:, :, :, 1], src[:, :, :, 0], ALU.subtract),
                           c_kvd)
                state["rot"] = t
                state["rkv_done"] = t
            elif kind == "kT":
                b = n % 2
                w, ps = pt_bank()
                pe.wait(state["rot"], t_id)
                t = transposes(ps, [krot[:, j, :] for j in range(4)], c_kv)
                state["krot_done"] = t
                t_kT[n] = pt_free[w] = hi_lo(ps, kTh[:, b, 0:512], kTl[:, b, 0:512], t, k_done.get(n - 2),
                                            c_kva, c_kvd)
            elif kind == "kn":
                b = n % 2
                w, ps = pt_bank()
                pe.wait(state["wk"], t_xT[0])
                terms = []
                for c in range(NC):
                    terms += split3(wkvh[:, c, :], wkvl[:, c, :], xTh[:, c, 0:64], xTl[:, c, 0:64])
                t = products(ps[:, 0:64], terms, c_kv)
                state["wkv_done"] = t
                act.wait(t, t_rot, k_done.get(n - 2))
                hi, lo = kTh[:, b, 512:576], kTl[:, b, 512:576]
                a = act.do(lambda e: e.activation(hi, ps[:, 0:64], ACT.Identity, scale=cs2[:, 0:1]), c_kva)
                dve.wait(a)
                pt_free[w] = dve.do(lambda e: e.scalar_tensor_tensor(
                    lo, ps[:, 0:64], cs2[:, 0:1], f(hi), ALU.mult, ALU.subtract), c_kvd)
                t_kn[n] = pt_free[w]
            elif kind == "vn":
                b = n % 2
                w, ps = pt_bank()
                pe.wait(state["wv"], t_xT[0])
                terms = []
                for c in range(NC):
                    terms += split3(xTh[:, c, 0:64], xTl[:, c, 0:64], wkvh[:, c, :], wkvl[:, c, :])
                t = products(ps[0:64, 0:128], terms, c_kv)
                state["wkv_done"] = t
                act.wait(t, v_done.get(n - 2), t_v4)
                act.do(lambda e: e.activation(v4a[0:64, b, :], ps[0:64, 0:128], ACT.Copy))
                a = act.do(lambda e: e.activation(v4b[0:64, b, :], ps[0:64, 0:128], ACT.Copy), c_kva)
                dve.wait(a, t_vn.get(n - 1))
                pt_free[w] = d = dve.do(lambda e: e.tensor_tensor(
                    vtmp[:, :], ps[0:64, 0:128], f(v4b[0:64, b, :]), ALU.subtract), c_kvd)
                sp.wait(d, v_done.get(n - 2))
                t_vn[n] = sp.do(lambda e: e.dma_start(f(v4a[64:128, b, :]), f(vtmp[:, :])), c_vn, 16)
            elif kind == "vs":
                b = n % 2
                act.wait(state["gv"], v_done.get(n - 2))
                a = act.do(lambda e: e.activation(vh[:, b], rkv[:, :, :], ACT.Copy), c_kva)
                pool.wait(a)
                t = pool.do(lambda e: e.tensor_tensor(vl[:, b], rkv[:, :, :], f(vh[:, b]), ALU.subtract), c_kvp)
                state["rkv_done"] = t
                t_v[n] = [t]
            elif kind == "xwq":
                split_weight(("wq", n), loaded, flat(wqh[:, n % 4]), flat(wql[:, n % 4]), wq_done[NH - 4 + n % 4])
            elif kind == "xwk":
                split_weight(("wk", n), loaded, flat(wkvh[:, :, :]), flat(wkvl[:, :, :]), state["wkv_done"])
            elif kind == "ctx":
                s, t_in = loaded
                w, ps = pt_bank()
                raw_free[s], t_ct[n] = token_tile(ps, None, [raws[s][:, 128 * c:128 * c + 128] for c in range(NC)],
                                                  t_in, CT + 128 * n, t_qp[125])
                pt_free[w] = t_ct[n]
            elif kind == "bias":
                s, t_in = loaded
                w, ps = pt_bank()
                pe.wait(t_in, t_id)
                raw_free[s] = t = pe.do(lambda e: e.transpose(ps[:, 0:48], raws[s][0:48, 0:128], ident[0:48, 0:48]),
                                        c_xtr)
                dve.wait(t)
                state["bqk"] = pt_free[w] = dve.do(lambda e: e.tensor_copy(bqk[:, :], ps[:, 0:48]), c_kvd)
            elif kind == "xt":
                w, ps = pt_bank()
                _, t_xT[n // 4] = token_tile(ps, None, [xacc[:, n, 128 * c:128 * c + 128] for c in range(NC)],
                                             t_x[n], 128 * n, None)
                pt_free[w] = t_xT[n // 4]
            elif kind == "stats":
                ts = list(range(2 * n, 2 * n + 2))
                ln_stats(ts, [t_addx[t] for t in ts])


        pre = [task("wq", 0)[2]()]
        t_c = load_rotation()
        pre += [task(*a)[2]() for a in (("wk", 0), ("wq", 1))]
        for q in range(1, 4):
            load_x(q)
        banks = [ps_o, big[0][:, 0, :], big[0][:, 1, :], big[1][:, 0, :], big[1][:, 1, :]]
        bank_free, turn = [None] * 5, [0]

        def x_tiles(q):
            for tt in range(4 * q, 4 * q + 4):
                b = turn[0] % 5
                turn[0] += 1
                _, t_xT[q] = token_tile(banks[b], bank_free[b], [xacc[:, tt, 128 * c:128 * c + 128] for c in range(NC)],
                                        t_x[tt], 128 * tt, None)
                bank_free[b] = t_xT[q]

        t_idx = key_rows()
        run_task("gk", 0, None)
        x_tiles(0)
        run_task("wq", 0, pre[0])
        t_rot = rotation(t_c)
        run_task("wk", 0, pre[1])

        plan = {}
        for g in range(G):
            s = 16 * g
            plan[s] = [("wo", 4 * g)]
            plan[s + 1] = [("wo", 4 * g + 1)]
            plan[s + 2] = [("wq", 4 * g + 2)]
            plan[s + 3] = [("wq", 4 * g + 3)]
            plan[s + 8] = [("wo", 4 * g + 2)]
            plan[s + 9] = [("wo", 4 * g + 3)]
            if g + 1 < G:
                plan[s + 4] = [("gk", g + 1), ("wk", g + 1)]
                plan[s + 5] = [("rot", g + 1), ("kn", g + 1), ("gv", g + 1)]
                plan[s + 6] = [("kT", g + 1)]
                plan[s + 7] = [("vs", g + 1)]
                plan[s + 10] = [("wv", g + 1)]
                plan[s + 11] = [("vn", g + 1)]
                plan[s + 12] = [("wq", 4 * g + 4)]
                plan[s + 13] = [("wq", 4 * g + 5)]
        for n, a in ((-1, ("xt", 12)), (-1, ("xt", 13)), (-1, ("vs", 0)), (0, ("xt", 14)), (1, ("xt", 15)),
                     (117, ("xwk", 0)), (118, ("xwq", 0)), (119, ("xwq", 1)), (122, ("bias", 0)),
                     (123, ("ctx", 0)), (124, ("ctx", 1)),
                     (125, ("ctx", 2)), (126, ("ctx", 3)),
                     (127, ("xwq", 2)), (128, ("xwq", 3))):
            plan.setdefault(n, []).append(a)
        order = [(s, a) for s in sorted(plan) for a in plan[s]]
        queue = [(s, task(*a)) for s, a in order]
        pending = {}
        nxt = [0]

        def prefetch(upto):
            while nxt[0] < len(queue) and queue[nxt[0]][0] <= upto:
                s, (kind, n, load) = queue[nxt[0]]
                pending[(kind, n)] = load()
                nxt[0] += 1

        UNITS = 128
        t_qp, t_q, t_s, t_max, t_exp, t_rec, t_p = {}, {}, {}, {}, {}, {}, {}
        t_phi, t_bank = {}, {}
        t_tr, t_plo, t_pv, t_olo, t_wod = {}, {}, {}, {}, {}
        t_addx = [None] * NT
        t_wop = {}

        def head(u):
            return 2 * (u // 8) + u % 2

        def qg(u):
            return (u % 8) // 2

        def q_pe(u, a=0, z=12):
            h, c0 = head(u), 512 * qg(u)
            pe.wait(t_wq[h], t_xT[qg(u)], m_free[0])
            terms = []
            for c in range(NC):
                terms += split3(wqh[:, h % 4, c, :], wql[:, h % 4, c, :],
                                xTh[:, c, c0:c0 + 512], xTl[:, c, c0:c0 + 512])
            t = products(ps_m, terms[a:z], c_q if z == 12 else None, first=a == 0, final=z == 12)
            if z == 12:
                wq_done[h] = t_qp[u] = t

        def q_out(u):
            t_q[u] = hi_lo(ps_m, qTh[:, u % 2], qTl[:, u % 2], t_qp[u], t_s.get(4 * (u - 2) + 3), c_qhi, c_qlo)
            m_free[0] = t_q[u]

        def s_pe(u, t):
            i, b = 4 * u + t, (head(u) // 4) % 2
            pe.wait(t_q[u], t_kT[head(u) // 4], t_kn[head(u) // 4], t_exp.get(i - 2))
            a, z = 128 * t, 128 * t + 128
            dst = ps_s[i % 2]
            terms = split3(qTh[:, u % 2, a:z], qTl[:, u % 2, a:z], kTh[:, b], kTl[:, b])
            for n, (l, r) in enumerate(terms):
                for k in range(2):
                    last = n == 2 and k == 1
                    tok = pe.do(lambda e, l=l, r=r, k=k, n=n: e.matmul(
                        dst[:, k, 0:HALF], l, r[:, HALF * k:HALF * k + HALF], start=n == 0, stop=n == 2),
                        c_s if last else None)
            t_s[i] = tok
            k_done[head(u) // 4] = tok

        def s_max(u, t):
            i = 4 * u + t
            dve.wait(t_s[i])
            t_max[i] = dve.do(lambda e: e.tensor_reduce(
                nmx[:, i % 8:i % 8 + 1], ps_s[i % 2][:, :, 0:HALF], AX.XY, ALU.max, negate=True), c_max)

        def s_exp(u, t):
            i = 4 * u + t
            act.wait(t_max[i], t_tr.get(5 * (u - 2) + 4))
            t_exp[i] = act.do(lambda e: e.activation(
                P[:, i % 8, 0:KEYS].rearrange("p (k n) -> p k n", k=2), ps_s[i % 2][:, :, 0:HALF], ACT.Exp,
                bias=nmx[:, i % 8:i % 8 + 1], scale=1.0, accum_out=rsum[:, i % 8:i % 8 + 1]), c_exp)

        def s_norm(u, t):
            i = 4 * u + t
            dve.wait(t_exp[i])
            dve.do(lambda e: e.tensor_copy(P[:, i % 8, KEYS:KEYS + 64], P[:, i % 8, 512:KEYS]), c_dup)
            t_rec[i] = dve.do(lambda e: e.reciprocal(rrec[:, i % 8:i % 8 + 1], rsum[:, i % 8:i % 8 + 1]), c_rec)
            pool.wait((c_dup, c_dup.n), t_rec[i])
            t_p[i] = pool.do(lambda e: e.tensor_scalar(
                P[:, i % 8, :], P[:, i % 8, :], rrec[:, i % 8:i % 8 + 1], 1.0, ALU.mult, ALU.mult), c_p)

        def tr_pe(u, j):
            k = 5 * u + j
            b, ps = pt_bank()
            t_bank[k] = b
            for t in range(4):
                src = P[:, (4 * u + t) % 8, 128 * j:128 * j + 128]
                pe.wait(t_p[4 * u + t])
                t_tr[k] = pe.do(lambda e, t=t, src=src: e.transpose(ps[:, 128 * t:128 * t + 128], src, ident[:, :]),
                                c_tr if t == 3 else None)

        def tr_hi(u, j):
            k = 5 * u + j
            act.wait(t_tr[k], t_pv.get(k - 2))
            t_phi[k] = act.do(lambda e: e.activation(pth[:, k % 2], ps_pt[t_bank[k]][:, :], ACT.Copy), c_phi)

        def tr_lo(u, j):
            k = 5 * u + j
            dve.wait(t_phi[k])
            t_plo[k] = pt_free[t_bank[k]] = dve.do(lambda e: e.tensor_tensor(
                ptl[:, k % 2], ps_pt[t_bank[k]][:, :], f(pth[:, k % 2]), ALU.subtract), c_plo)

        def pv_pe(u, j):
            k, g = 5 * u + j, head(u) // 4
            b = g % 2
            pe.wait(t_plo[k], t_v[g], t_vn[g])
            if j == 0:
                pe.wait(t_olo.get(u - 1))
            h, l = pth[:, k % 2], ptl[:, k % 2]
            if j < 4:
                terms = [(vh[:, b, j], h), (vl[:, b, j], h), (vh[:, b, j], l)]
            else:
                terms = [(v4a[:, b], h), (v4b[:, b], l)]
            t_pv[k] = products(ps_o, terms, c_pv, first=j == 0, final=j == 4)
            v_done[g] = t_pv[k]

        def o_out(u):
            t_olo[u] = hi_lo(ps_o, oh[:, u % 3], ol[:, u % 3], t_pv[5 * u + 4], t_wod.get(u - 3), c_ohi, c_olo)

        m_banks = [ps_m, ps_s[0][:, 0, :], ps_s[0][:, 1, :], ps_o]

        def m_bank(u, t):
            return m_banks[t] if u == UNITS - 1 else ps_m

        def wo_pe(u, t):
            a, z, tt = 128 * t, 128 * t + 128, 4 * qg(u) + t
            pe.wait(t_olo[u], t_wo[head(u - 1)], t_wo[head(u)], m_free[0] if m_bank(u, t) is ps_m else t_exp[4 * u + 3])
            terms = []
            for w in (u - 1, u):
                h = head(w)
                terms += split3(oh[:, w % 3, a:z], ol[:, w % 3, a:z], woh[:, h % 3], wol[:, h % 3])
            tok = products(m_bank(u, t), terms, c_wo)
            for w in (u - 1, u):
                t_wod[w] = tok
                wo_done[head(w)] = tok
            t_wop[tt] = tok

        def wo_add(u, t):
            tt = 4 * qg(u) + t
            dve.wait(t_wop[tt], t_addx[tt])
            t_addx[tt] = dve.do(lambda e: e.tensor_tensor(
                xacc[:, tt, :], m_bank(u, t), xacc[:, tt, :], ALU.add), c_add)
            if m_bank(u, t) is ps_m:
                m_free[0] = t_addx[tt]

        def wo_steps(u):
            w, half = (u - 1, 0) if u % 2 == 0 else (u - 2, 1)
            return [(w, 2 * half), (w, 2 * half + 1)] if 1 <= w < UNITS else []

        def real(u):
            return 0 <= u < UNITS

        q_pe(0)
        run_task("kn", 0, None)
        q_out(0)
        run_task("wq", 1, pre[2])
        run_task("rot", 0, None)
        q_pe(1)
        run_task("kT", 0, None)
        x_tiles(1)
        run_task("gv", 0, None)
        run_task("wv", 0, task("wv", 0)[2]())
        x_tiles(2)
        run_task("vn", 0, None)
        pe.wait(bank_free)
        prefetch(1)
        t_first = {}
        t_ln = [None] * NT

        def rows(tiles):
            t = ln_rows(tiles)
            for tt in tiles:
                t_ln[tt] = t

        def first_keys(s):
            ps, c0 = big[1][:, s, :], CT + 256 * s
            pe.wait(t_exp[4 * UNITS - 1], t_w[("wk", 0)], t_ct[2 * s], t_ct[2 * s + 1])
            terms = []
            for c in range(NC):
                terms += split3(wkvh[:, c, :], wkvl[:, c, :], xTh[:, c, c0:c0 + 256], xTl[:, c, c0:c0 + 256])
            t_first[s] = products(ps[:, 0:256], terms, c_kv)

        on_pe = ("wq", "wo", "wk", "wv", "kn", "vn", "kT", "ctx", "xt")
        for u in range(-1, UNITS + 2):
            nxt_, cur, todo = real(u + 1), real(u), wo_steps(u)
            prefetch(u + 2)

            def new(fn, t):
                if nxt_:
                    fn(u + 1, t)

            def old(fn, j):
                if cur:
                    fn(u, j)

            def wo_do(fn, i):
                if todo:
                    fn(*todo[i])

            if u >= UNITS - 1 and u - UNITS + 1 < 2:
                first_keys(u - UNITS + 1)
            new(s_pe, 0)
            if real(u + 2):
                q_out(u + 2)
            old(tr_hi, 1)
            new(s_max, 0)
            old(tr_lo, 1)
            new(s_exp, 0)
            old(pv_pe, 0)
            wo_do(wo_pe, 0)
            new(s_norm, 0)
            old(tr_pe, 2)
            wo_do(wo_add, 0)
            if u == UNITS - 1:
                run_task("stats", 0, None)
            new(s_pe, 1)
            old(tr_hi, 2)
            new(s_max, 1)
            old(tr_lo, 2)
            new(s_exp, 1)
            old(pv_pe, 1)
            old(tr_pe, 3)
            wo_do(wo_pe, 1)
            new(s_norm, 1)
            old(tr_hi, 3)
            old(tr_lo, 3)
            old(tr_pe, 4)
            new(s_pe, 2)
            wo_do(wo_add, 1)
            if u == UNITS - 1:
                run_task("stats", 1, None)
            new(s_max, 2)
            old(pv_pe, 2)
            old(tr_hi, 4)
            new(s_exp, 2)
            new(s_pe, 3)
            old(tr_lo, 4)
            new(s_norm, 2)
            new(s_max, 3)
            new(s_exp, 3)
            old(pv_pe, 3)
            new(s_norm, 3)
            for kind, n in plan.get(u, []):
                run_task(kind, n, pending.pop((kind, n)))
            fill = 0 if any(kind in on_pe for kind, n in plan.get(u, [])) else 2
            if fill and real(u + 3):
                q_pe(u + 3, 0, fill)
            old(pv_pe, 4)
            if real(u + 3):
                q_pe(u + 3, fill, 9)
            if cur:
                o_out(u)
            if u == UNITS - 1:
                ln_root([0, 1, 2, 3])
                rows([0, 1])
            new(tr_pe, 0)
            new(tr_hi, 0)
            new(tr_lo, 0)
            if real(u + 3):
                q_pe(u + 3, 9, 12)
            new(tr_pe, 1)

        def barrier(engines, but=()):
            toks = [(c, c.n) for c in counts if c.n and c not in but]
            for e in engines:
                e.wait(toks)

        counts = ([c_init, c_cst, c_idx, c_bob, c_pcol, c_xtr, c_xhi, c_xlo, c_gk, c_gv, c_wtr, c_whi, c_wlo, c_wlp, c_kv, c_kvd, c_kva, c_kvp, c_vn,
                   c_q, c_qhi, c_qlo, c_s, c_max, c_exp, c_rec, c_dup, c_p, c_tr, c_phi, c_plo, c_pv, c_ohi, c_olo,
                   c_wo, c_add, c_ln, c_lna, c_bo, c_sub, c_sub2, c_sum, c_ff, c_ffa, c_ffd] + c_raw + c_x)
        barrier((dve, act, pool), (c_add, c_ln, c_lna))
        one.close()

        two = ExitStack()
        HT = NT // 2
        wkh2, wkl2 = pair("xwk", [128, 512], two)
        wvh2, wvl2 = pair("xwv", [128, NC, 2, 128], two)
        uh, ul = pair("xwo", [128, 4, 512], two)
        k2 = sb("xk", [128, 16, 2, 64], F32R, two)
        v2h, v2l = pair("xv", [128, HT, 256], two)
        q2h, q2l = pair("xq", [128, 4, 2, 128], two)
        sB = sb("sB", [128, 2, 256], F32, two)
        P2 = sb("P2", [128, 2, 256], F32, two)
        p2h, p2l = pair("xp", [128, 512], two)
        o2h, o2l = pair("xo", [128, 8, 128], two)
        rawb = sb("rawb", [128, 3, 512], F32, two)
        bob = sb("bob", [128, 512], F32, two)
        mx2 = sb("mx2", [128, 8], F32, two)
        sm2 = sb("sm2", [128, 8], F32, two)

        ps_q = [big[0][:, 0, :], big[0][:, 1, :]]
        ps_sc = big[1]
        ps_ov = [big[2][:, 0, :], big[2][:, 1, :]]
        ps_tp = bank[0][:, :]
        ps_w = bank[1][:, :]

        GG = 2 * G
        STEPS = 4 * GG

        def blocks_at(g, s):
            if s == 0:
                return [("wo", 4 * g + j) for j in range(4)]
            if g == GG - 1:
                return {1: [("fw", 0), ("fw", 1)], 2: [("fw", 2), ("fw", 3), ("fa", 0), ("fb", 0)]}.get(s, [])
            if s == 1:
                a = [("wk", g + 2)] if g + 2 < GG else []
                return a + ([("wv", g + 2), ("wv", g + 3)] if g % 2 == 0 and g + 2 < GG else [])
            if s == 2:
                return [("wq", 4 * (g + 1) + j) for j in range(4)]
            return []

        def tiles_at(g, s):
            return [HT + 2 * s, HT + 2 * s + 1] if g == G - 1 else []

        line = [("wv", 0), ("wv", 1)] + [("ctx", t) for t in range(4, HT)] + [("wk", 1)]
        for n in range(STEPS):
            line += [("ctx", t) for t in tiles_at(n // 4, n % 4)] + blocks_at(n // 4, n % 4)
        fetched = {}
        at = [0, 0]

        def load2(kind, n):
            if kind == "wq":
                return load_raw(as_blocks, wq2_v[n % NH])
            if kind == "wk":
                return load_raw(as_blocks, wkv2_v[n % G])
            if kind == "wv":
                return load_raw(as_blocks, wkv2_v[G + n % G])
            if kind == "wo":
                return load_raw(as_rows, wo2_v[n % NH])
            if kind == "fw":
                return load_raw(as_rows, fW[128 * n:128 * n + 128, :])
            if kind == "fb":
                return load_raw(as_rows, fB.rearrange("x r o -> (x r) o"))
            if kind == "fa":
                return load_fa()
            return load_raw(as_rows, cf[128 * n:128 * n + 128, :])

        def ahead(upto):
            while at[0] < min(len(line), upto):
                fetched[line[at[0]]] = load2(*line[at[0]])
                at[0] += 1

        def take(kind, n):
            assert line[at[1]] == (kind, n), (line[at[1]], kind, n)
            ahead(at[1] + len(raws))
            at[1] += 1
            return fetched.pop((kind, n))

        def load_fa():
            r = raw_slot()
            for c in range(NC):
                t = sp.do(lambda e, c=c: e.dma_start(
                    raws[r][:, 128 * c:128 * c + 128].rearrange("p (x r) -> p x r", r=16),
                    fA[:, 128 * c:128 * c + 128, :].rearrange("x p r -> p x r")), c_raw[r], 16)
            return r, t

        def wk_at(g):
            return (wkh2[:, :], wkl2[:, :]) if g % 2 else (flat(wkvh[:, :, :]), flat(wkvl[:, :, :]))

        FA = CT + 512

        def weight2(kind, n):
            loaded = take(kind, n)
            if kind == "fw":
                s, t_in = loaded
                free, b, ps = tile_bank(n, False)
                raw_free[s], t_w[(kind, n)] = token_tile(
                    ps, None, [raws[s][:, 128 * c:128 * c + 128] for c in range(NC)], t_in, CT + 128 * n, ct_done[n // 2])
                free[b] = t_w[(kind, n)]
                return
            if kind == "fa":
                split_weight((kind, n), loaded, xTh[:, :, FA:FA + 128], xTl[:, :, FA:FA + 128], ct_done[2], True)
                return
            if kind == "fb":
                split_weight((kind, n), loaded, *wk_at(0), w_done[("wk", GG - 2)])
                return
            if kind == "wq":
                hi, lo, old = flat(wqh[:, n % 4]), flat(wql[:, n % 4]), n - 4
            elif kind == "wo":
                hi, lo, old = uh[:, n % 4], ul[:, n % 4], n - 4
            elif kind == "wk":
                (hi, lo), old = wk_at(n), n - 2
            else:
                hi, lo, old = wvh2[:, :, n % 2, :], wvl2[:, :, n % 2, :], n - 2
            split_weight((kind, n), loaded, hi, lo, w_done.get((kind, old)), kind == "wv",
                         (dve, c_wlo) if kind == "wo" and n % 2 else None)

        q_free, q_turn, q_ring = [t_addx[13], t_addx[14], pt_free[0], pt_free[1], None, None, t_addx[15], t_addx[12]], [0], [8]
        q_banks = ps_q + [ps_tp, ps_w, ps_sc[:, 0, :], ps_sc[:, 1, :]] + ps_ov
        ov_free = [None, None]

        def q_bank():
            b = q_turn[0] % q_ring[0]
            q_turn[0] += 1
            pe.wait(q_free[b])
            return b, q_banks[b]

        def tile_bank(tt, over):
            if over:
                pe.wait(ov_free[tt % 2])
                return ov_free, tt % 2, ps_ov[tt % 2]
            b, ps = q_bank()
            return q_free, b, ps

        t_x2 = [None] * NT
        x2_done, ct_done = [None] * 4, [None] * 4

        def ctx_tile(tt, over=False):
            s, t_in = take("ctx", tt)
            i = tt % HT
            free, b, ps = tile_bank(tt, over)
            raw_free[s], t_ct[tt] = token_tile(ps, None, [raws[s][:, 128 * c:128 * c + 128] for c in range(NC)], t_in,
                                               CT + 128 * i, ct_done[i // 2])
            free[b] = t_ct[tt]

        def x2_tile(tt, t_in, over=False):
            i = tt % HT
            free, b, ps = tile_bank(tt, over)
            t, t_x2[tt] = token_tile(ps, None, [xacc[:, tt, 128 * c:128 * c + 128] for c in range(NC)], t_in,
                                     128 * i, x2_done[i // 2])
            free[b] = t_x2[tt]
            pool.wait(t, t_bob)
            t_addx[tt] = pool.do(lambda e: e.tensor_tensor(xacc[:, tt, :], xacc[:, tt, :], bob[:, :], ALU.add), c_bo)

        t_x3, t_x3t, t_l3 = [None] * NT, [None] * NT, [None] * NT

        def normal3(tiles):
            ln_stats(tiles, [t_addx[t] for t in tiles])
            ln_root(tiles)
            t = ln_rows(tiles)
            for tt in tiles:
                t_l3[tt] = t

        def x3_tile(tt, t_free, over=False):
            free, b, ps = tile_bank(tt, over)
            t_x3t[tt], t_x3[tt] = token_tile(ps, None, [xacc[:, tt, 128 * c:128 * c + 128] for c in range(NC)],
                                             t_l3[tt], 128 * (tt % 8), t_free)
            free[b] = t_x3[tt]

        def rows2(g, s):
            return [HT * (g // G) + 2 * s, HT * (g // G) + 2 * s + 1]

        t_q2, t_k2, t_v2, t_s2, t_p2, t_pt2, t_pv2, t_o2 = {}, {}, {}, {}, {}, {}, {}, {}
        t_wo2, t_tr2 = {}, {}
        w_free = [None]

        def qproj(n, p):
            g, s = n // 4, n % 4
            c0 = 256 * s
            b, ps = q_bank()
            pe.wait([t_x2[t] for t in rows2(g, s)])
            for j in range(2):
                h = 4 * g + 2 * p + j
                pe.wait(t_w[("wq", h)])
                terms = []
                for c in range(NC):
                    terms += split3(wqh[:, h % 4, c], wql[:, h % 4, c], xTh[:, c, c0:c0 + 256], xTl[:, c, c0:c0 + 256])
                t = products(ps[:, 256 * j:256 * j + 256], terms, c_q)
                w_done[("wq", h)] = t
            x2_done[s] = t
            views = []
            act.wait(t, t_s2.get(n - 1), t_bqk)
            for j in range(2):
                h = (4 * g + 2 * p + j) % NH
                hi, lo = q2h[:, :, p, 64 * j:64 * j + 64], q2l[:, :, p, 64 * j:64 * j + 64]
                src = ps[:, 256 * j:256 * j + 256].rearrange("p (b i) -> p b i", i=64)
                views.append((hi, lo, src, bqk[:, h:h + 1]))
                a = act.do(lambda e, hi=hi, src=src, h=h: e.activation(
                    hi, src, ACT.Identity, bias=bqk[:, h:h + 1]), c_qhi)
            dve.wait(a)
            for hi, lo, src, bq in views:
                t = dve.do(lambda e, hi=hi, lo=lo, src=src, bq=bq: e.scalar_tensor_tensor(
                    lo, src, bq, f(hi), ALU.add, ALU.subtract), c_qlo)
            q_free[b] = t_q2[n] = t

        def kproj(g, s):
            c0 = CT + 256 * s
            wh, wl = wk_at(g)
            if g == 0 and s in t_first:
                b, t = 4 + s, t_first[s]
                ps = q_banks[b]
            else:
                b, ps = q_bank()
                pe.wait(t_w[("wk", g)], [t_ct[t] for t in rows2(g, s)])
                terms = []
                for c in range(NC):
                    w = slice(128 * c, 128 * c + 128)
                    terms += split3(wh[:, w], wl[:, w], xTh[:, c, c0:c0 + 256], xTl[:, c, c0:c0 + 256])
                t = products(ps[:, 0:256], terms, c_kv)
            w_done[("wk", g)] = t
            ct_done[s] = t
            src = ps[:, 0:256].rearrange("p (b i) -> p b i", i=64)
            hi, lo = k2[:, 4 * s:4 * s + 4, 0, :], k2[:, 4 * s:4 * s + 4, 1, :]
            bk = bqk[:, 32 + g % G:33 + g % G]
            act.wait(t, t_s2.get(4 * (g - 1) + s), t_bqk)
            a = act.do(lambda e: e.activation(hi, src, ACT.Identity, bias=bk), c_kva)
            dve.wait(a)
            q_free[b] = t_k2[(g, s)] = dve.do(lambda e: e.scalar_tensor_tensor(
                lo, src, bk, f(hi), ALU.add, ALU.subtract), c_kvd)

        def vproj(g, s):
            b, ps = q_bank()
            pe.wait(t_w[("wv", g)], t_w[("wv", g + 1)], [t_ct[t] for t in rows2(g, s)])
            for i in range(2):
                a0 = CT + 256 * s + 128 * i
                terms = []
                for c in range(NC):
                    terms += split3(xTh[:, c, a0:a0 + 128], xTl[:, c, a0:a0 + 128], flat(wvh2[:, c]), flat(wvl2[:, c]))
                t = products(ps[:, 256 * i:256 * i + 256], terms, c_kv)
            w_done[("wv", g)] = w_done[("wv", g + 1)] = t
            ct_done[s] = t
            q_free[b] = t_v2[(g, s)] = t_v2[(g + 1, s)] = hi_lo(
                ps, flat(v2h[:, 2 * s:2 * s + 2, :]), flat(v2l[:, 2 * s:2 * s + 2, :]),
                t, t_pv2.get(4 * (g - 1) + s), c_kva, c_kvd)

        def scores2(n):
            g, s = n // 4, n % 4
            pe.wait(t_q2[n], t_k2[(g, s)], t_p2.get(("add", n - 1)))
            tok = []
            for bp in range(2):
                for p in range(2):
                    for bo in range(2):
                        i = 2 * bp + bo
                        kk = flat(k2[:, 4 * s + i])
                        c0 = 256 * p + 128 * bo
                        t = products(ps_sc[:, bp, c0:c0 + 128], [(q2h[:, i, p], kk), (q2l[:, i, p], kk)], c_s)
                tok.append(t)
            t_s2[n] = t
            for bp in range(2):
                ab = ps_sc[:, bp, :].rearrange("p (x a k) -> p x a k", a=2, k=64)
                low = sB[:, bp].rearrange("p (x k) -> p x k", k=64)
                dst = P2[:, bp].rearrange("p (x k) -> p x k", k=64)
                act.wait(tok[bp], t_p2.get(("add", n - 1)))
                a = act.do(lambda e, low=low, ab=ab: e.activation(low, ab[:, :, 1, :], ACT.Copy), c_sub)
                dve.wait(a, t_tr2.get(n - 1))
                d = dve.do(lambda e, low=low, ab=ab, dst=dst: e.tensor_tensor(dst, ab[:, :, 0, :], low, ALU.add), c_sub2)
            t_p2[("add", n)] = d
            pv = flat(P2[:, :, :]).rearrange("p (x k) -> p x k", k=64)
            dve.wait(d)
            m = dve.do(lambda e: e.tensor_reduce(mx2[:, :], pv, AX.X, ALU.max), c_max)
            dve.wait(m)
            d = dve.do(lambda e: e.tensor_tensor(
                pv, pv, mx2[:, :].unsqueeze(2).to_broadcast([128, 8, 64]), ALU.subtract), c_max)
            act.wait(d)
            t_p2[("exp", n)] = act.do(lambda e: e.activation(
                flat(P2[:, :, :]), flat(P2[:, :, :]), ACT.Exp, scale=SCALE), c_exp)

        def softmax2(n):
            pv = flat(P2[:, :, :]).rearrange("p (x k) -> p x k", k=64)
            dve.wait(t_p2[("exp", n)])
            a = dve.do(lambda e: e.tensor_reduce(sm2[:, :], pv, AX.X, ALU.add), c_sum)
            dve.wait(a)
            a = dve.do(lambda e: e.reciprocal(sm2[:, :], sm2[:, :]), c_rec)
            pool.wait(a)
            t_p2[n] = pool.do(lambda e: e.tensor_tensor(
                pv, pv, sm2[:, :].unsqueeze(2).to_broadcast([128, 8, 64]), ALU.mult), c_p)

        def turn2(n):
            pe.wait(t_p2[n], t_pt2.get(n - 1))
            t_tr2[n] = transposes(ps_tp, [flat(P2[:, :, :])[:, 128 * b:128 * b + 128] for b in range(4)], c_tr)
            t_pt2[n] = hi_lo(ps_tp, p2h[:, :], p2l[:, :], t_tr2[n], t_pv2.get(n - 1), c_phi, c_plo)

        def values2(n):
            g, s = n // 4, n % 4
            pe.wait(t_pt2[n], t_v2[(g, s)], ov_free)
            for bp in range(2):
                for par in range(2):
                    r = slice(64 * par, 64 * par + 64)
                    cc = slice(256 * bp, 256 * bp + 256)
                    d = slice(128 * (g % 2), 128 * (g % 2) + 128)
                    t = products(ps_ov[par][:, cc], split3(v2h[r, 2 * s + bp, d], v2l[r, 2 * s + bp, d],
                                                           p2h[r, cc], p2l[r, cc]), c_pv)
            t_pv2[n] = t
            bv = bqk[:, 40 + g % G:41 + g % G]
            act.wait(t, t_wo2.get(n - 1), t_bqk)
            for par in range(2):
                src = ps_ov[par].rearrange("p (x i) -> p x i", i=64)
                hi, lo = o2h[:, :, 64 * par:64 * par + 64], o2l[:, :, 64 * par:64 * par + 64]
                a = act.do(lambda e, hi=hi, src=src: e.activation(hi, src, ACT.Identity, bias=bv), c_ohi)
                dve.wait(a)
                ov_free[par] = t_o2[n] = dve.do(lambda e, hi=hi, lo=lo, src=src: e.scalar_tensor_tensor(
                    lo, src, bv, f(hi), ALU.add, ALU.subtract), c_olo)

        def wo2(n, i):
            if n < 0:
                return
            if n == STEPS - 1:
                b, ps = q_bank()
                free = q_free
            else:
                b, ps, free = 0, ps_w, w_free
            g, s = n // 4, n % 4
            tt = rows2(g, s)[i]
            pe.wait(t_o2[n], free[b])
            for j in range(4):
                pe.wait(t_w[("wo", 4 * g + j)])
                t = products(ps, split3(o2h[:, 4 * i + j], o2l[:, 4 * i + j], uh[:, j], ul[:, j]),
                             c_wo if j == 3 else None, first=j == 0, final=j == 3)
            for j in range(4):
                w_done[("wo", 4 * g + j)] = t
            t_wo2[n] = t
            dve.wait(t, t_addx[tt])
            free[b] = t_addx[tt] = dve.do(lambda e: e.tensor_tensor(
                xacc[:, tt, :], ps, xacc[:, tt, :], ALU.add), c_add)

        ps_u = bank[0][:, :]

        def low_rank_pe(q, t_free):
            c0 = 512 * (q % 2)
            pe.wait([t_x3[t] for t in range(4 * q, 4 * q + 4)], t_w[("fa", 0)], t_free, t_pt2[STEPS - 1])
            terms = []
            for c in range(NC):
                terms += split3(xTh[:, c, FA:FA + 128], xTl[:, c, FA:FA + 128],
                                xTh[:, c, c0:c0 + 512], xTl[:, c, c0:c0 + 512])
            return products(ps_u, terms, c_ff)

        raw_n[0] %= 3
        first = raw_n[0]
        ahead(3)
        barrier((sp,))
        raws[:] = [raws[(first + i) % 3] for i in range(3)] + [rawb[:, i, :] for i in range(3)]
        order = [(first + i) % 3 for i in range(3)]
        raw_free[:3] = [raw_free[i] for i in order]
        c_raw[:3] = [c_raw[i] for i in order]
        for i, k in enumerate(line[:3]):
            fetched[k] = (i, fetched[k][1])
        raw_n[0] = 3
        t_bob = sp.do(lambda e: e.dma_start(bob[:, :], xbo.rearrange("(a d) -> a d", a=1).to_broadcast([128, 512])),
                      c_bob, 16)
        t_pcol = sp.do(lambda e: e.dma_start(
            pcol[:, :], fp.rearrange("(x o) -> x o", o=1).unsqueeze(1).to_broadcast([8, 16, 1]),
            allow_slow_non_contiguous=True), c_pcol, 16)
        t_bqk = state["bqk"]
        kproj(0, 0)
        kproj(0, 1)
        for tt in (0, 1):
            x2_tile(tt, t_ln[tt])
        weight2("wv", 0)
        weight2("wv", 1)
        rows([2, 3])
        qproj(0, 0)
        ctx_tile(4)
        ctx_tile(5)
        qproj(0, 1)
        run_task("stats", 2, None)
        run_task("stats", 3, None)
        ln_root([4, 5, 6, 7])
        for tt in (2, 3):
            x2_tile(tt, t_ln[tt])
        vproj(0, 0)
        rows([4, 5])
        kproj(0, 2)
        ctx_tile(6)
        ctx_tile(7)
        vproj(0, 1)
        rows([6, 7])
        for tt in (4, 5):
            x2_tile(tt, t_ln[tt])
        vproj(0, 2)
        weight2("wk", 1)
        pe.wait(q_free[2:])
        q_ring[0] = 2

        for n in range(STEPS):
            g, s = n // 4, n % 4
            work = blocks_at(g, s)
            fresh = tiles_at(g, s)
            last, early = n == STEPS - 1, n in (STEPS - 3, STEPS - 2)
            scores2(n)
            wo2(n - 1, 0)
            if n == 0:
                for tt in (6, 7):
                    x2_tile(tt, t_ln[tt], True)
            for tt in fresh:
                ctx_tile(tt, True)
            softmax2(n)
            if not last:
                qproj(n + 1, 0)
                qproj(n + 1, 1)
            else:
                normal3(rows2(g, 0))
                wo2(n - 1, 1)
                for tt in (0, 1):
                    x3_tile(tt, x2_done[0])
            for tt in fresh:
                x2_tile(tt, t_ln[tt], True)
            turn2(n)
            if n == 0:
                kproj(0, 3)
            if not last:
                wo2(n - 1, 1)
            else:
                for tt in (2, 3):
                    x3_tile(tt, x2_done[1])
            if not early and not last:
                for a in work[:2]:
                    weight2(*a)
            values2(n)
            if early:
                for a in work:
                    weight2(*a)
            if last:
                normal3(rows2(g, 1))
            if n == 0:
                vproj(0, 3)
            if g + 1 < GG:
                kproj(g + 1, s)
                if g % 2 == 1:
                    vproj(g + 1, s)
            if not early and not last:
                for a in work[2:]:
                    weight2(*a)
            if 4 <= n < 8:
                ts = [HT + 2 * n - 8, HT + 2 * n - 7]
                ln_stats(ts, [t_addx[t] for t in ts])
                ln_root(ts)
                rows(ts)
            if g == G + 1:
                normal3(rows2(0, s))
        t_ur = low_rank_pe(0, None)
        x3_tile(4, x2_done[2])
        wo2(STEPS - 1, 0)
        wo2(STEPS - 1, 1)
        pe.wait(t_p2[("add", STEPS - 1)], ov_free, w_free)
        barrier((dve, act, pool, sp))
        two.close()

        three = ExitStack()
        fbb = sb("fbb", [128, 512], F32, three)
        uTh, uTl = pair("uT", [128, 512], three)
        z = sb("z", [128, 2, 512], F32, three)
        junk = sb("junk", [128, 2, 512], F32, three)
        gm_m = sb("gm_m", [128, 2, 512], F32, three)
        nrm = sb("nrm", [128, NT, 2], F32, three)
        nz = sb("nz", [128, NT, 2], F32, three)
        gam = sb("gam", [128, NT], F32, three)

        t_fbb = sp.do(lambda e: e.dma_start(fbb[:, :], fb.rearrange("(a d) -> a d", a=1).to_broadcast([128, 512])),
                      c_fbb, 16)
        ps_z = [big[1][:, 0, :], big[1][:, 1, :]]
        ps_mm = [big[2][:, 0, :], big[2][:, 1, :], bank[1][:, :]]
        z_free, mm_free, zs_free = [None, None], [None] * 3, [None, None]
        t_u, u_free, uslot = {}, None, None
        t_zz, t_nz, t_res, x3_done = {}, {}, {}, {}

        def low_rank_out(t):
            act.wait(t, uslot, t_pcol)
            a = act.do(lambda e: e.activation(uTh[:, :], ps_u, ACT.Identity, scale=pcol[:, 0:1]), c_ffa)
            dve.wait(a)
            return dve.do(lambda e: e.scalar_tensor_tensor(
                uTl[:, :], ps_u, pcol[:, 0:1], f(uTh[:, :]), ALU.mult, ALU.subtract), c_ffd)

        def z_pe(tt):
            b, s = tt % 2, slice(128 * (tt % 8), 128 * (tt % 8) + 128)
            pe.wait(z_free[b], t_x3[tt], [t_w[("fw", o)] for o in range(4)])
            terms = []
            for c in range(NC):
                terms += split3(xTh[:, c, s], xTl[:, c, s], xTh[:, c, CT:CT + 512], xTl[:, c, CT:CT + 512])
            x3_done[tt] = products(ps_z[b], terms, c_ff)

        def z_out(tt):
            b = tt % 2
            dve.wait(x3_done[tt], zs_free[b], t_fbb)
            z_free[b] = t_zz[tt] = dve.do(lambda e: e.tensor_tensor(z[:, b, :], ps_z[b], fbb[:, :], ALU.add), c_ffd)
            pool.wait(t_zz[tt], t_x3t[tt])
            t_res[tt] = pool.do(lambda e: e.tensor_tensor(
                xacc[:, tt, :], xacc[:, tt, :], z[:, b, :], ALU.add), c_bo)

        def m_pe(tt):
            mb, us = tt % 3, slice(128 * (tt % 4), 128 * (tt % 4) + 128)
            pe.wait(t_u[tt // 4], mm_free[mb], t_w[("fb", 0)])
            return products(ps_mm[mb], split3(uTh[:, us], uTl[:, us], flat(wkvh[:, :, :]), flat(wkvl[:, :, :])), c_ff)

        def norms(tt, t):
            b, mb = tt % 2, tt % 3
            act.wait(t_zz[tt], t_nz.get(tt - 1))
            act.do(lambda e: e.activation(junk[:, 0, :], z[:, b, :], ACT.Square, accum_out=nrm[:, tt, 0:1]), c_ffa)
            act.wait(t)
            a = act.do(lambda e: e.activation(junk[:, 1, :], ps_mm[mb], ACT.Square, accum_out=nrm[:, tt, 1:2]), c_ffa)
            act.wait(a)
            t_nz[tt] = act.do(lambda e: e.activation(nz[:, tt, :], nrm[:, tt, :], ACT.Sqrt), c_ffa)
            zs_free[b] = [t_nz[tt], t_res[tt]]

        def mix(tt):
            mb = tt % 3
            n0, n1, gm = nz[:, tt, 0:1], nz[:, tt, 1:2], gam[:, tt:tt + 1]
            dve.wait(t_nz[tt])
            d = dve.do(lambda e: e.tensor_scalar(n1, n1, 1e-6, None, ALU.add), c_ffd)
            yield
            dve.wait(d)
            d = dve.do(lambda e: e.reciprocal(n1, n1), c_ffd)
            yield
            dve.wait(d)
            d = dve.do(lambda e: e.scalar_tensor_tensor(gm, n0, 0.5, n1, ALU.mult, ALU.mult), c_ffd)
            yield
            dve.wait(d)
            d = dve.do(lambda e: e.tensor_scalar(gm, gm, 1.0, None, ALU.min), c_ffd)
            yield
            if tt >= NT - 3:
                dve.wait(d, t_res[tt])
                mm_free[mb] = t_addx[tt] = dve.do(lambda e: e.scalar_tensor_tensor(
                    xacc[:, tt, :], ps_mm[mb], gm, xacc[:, tt, :], ALU.mult, ALU.add), c_add)
                return
            b = tt % 2
            act.wait(d, t_addx[tt - 2] if tt >= 2 else None)
            mm_free[mb] = a = act.do(lambda e: e.activation(gm_m[:, b, :], ps_mm[mb], ACT.Copy, scale=gm), c_ffa)
            pool.wait(a, t_res[tt])
            t_addx[tt] = pool.do(lambda e: e.tensor_tensor(
                xacc[:, tt, :], xacc[:, tt, :], gm_m[:, b, :], ALU.add), c_bo)

        def measure(tiles):
            a, b = tiles[0], tiles[-1] + 1
            dve.wait([t_addx[t] for t in tiles])
            for tt in tiles:
                t = dve.do(lambda e, tt=tt: e.bn_stats(stat[:, tt, :], xacc[:, tt, :]), c_ln)
                yield
            dve.wait(t)
            for tt in tiles:
                t = dve.do(lambda e, tt=tt: e.bn_aggr(mv[:, tt, :], stat[:, tt, :]), c_ln)
            yield
            dve.wait(t)
            t = dve.do(lambda e: e.tensor_scalar(mv[:, a:b, 1], mv[:, a:b, 1], LN_EPS, None, ALU.add), c_ln)
            for tt in tiles:
                t_stat[tt] = t
            ln_root(tiles)

        def finish(tiles):
            a, b = tiles[0], tiles[-1] + 1
            dve.wait([t_rstd[t] for t in tiles])
            t = dve.do(lambda e: e.reciprocal(rstd[:, a:b], rstd[:, a:b]), c_ln)
            yield
            dve.wait(t)
            for tt in tiles:
                t = dve.do(lambda e, tt=tt: e.tensor_scalar(
                    xacc[:, tt, :], xacc[:, tt, :], mv[:, tt, 0:1], rstd[:, tt:tt + 1],
                    ALU.subtract, ALU.mult), c_ln)
                yield
            sp.wait(t)
            t_out.append(sp.do(lambda e: e.dma_start(
                of[128 * a:128 * b, :].rearrange("(t p) d -> p t d", p=128), xacc[:, a:b, :]), c_out, 16))

        def in_turn(*parts):
            parts = list(parts)
            while parts:
                for p in list(parts):
                    try:
                        next(p)
                    except StopIteration:
                        parts.remove(p)

        t_out = []
        u_free = t_u[0] = low_rank_out(t_ur)
        for tt in range(NT):
            q = tt // 4
            if tt + 5 < NT:
                x3_tile(tt + 5, x3_done.get(tt - 3))
            z_pe(tt)
            parts = [mix(tt - 2)] if tt >= 2 else []
            if tt >= 4 and tt % 2 == 0:
                parts.append(measure([tt - 4, tt - 3]))
            if tt >= 5 and tt % 2 == 1:
                parts.append(finish([tt - 5, tt - 4]))
            in_turn(*parts)
            t_m = m_pe(tt)
            uslot = t_m
            z_out(tt)
            norms(tt, t_m)
            if tt < 2:
                normal3([12 + 2 * tt, 13 + 2 * tt])
            if tt % 4 == 3 and q + 1 < 4:
                u_free = t_u[q + 1] = low_rank_out(low_rank_pe(q + 1, u_free))
        in_turn(measure([NT - 4, NT - 3]), mix(NT - 2))
        in_turn(mix(NT - 1), measure([NT - 2]), finish([NT - 4, NT - 3]))
        in_turn(measure([NT - 1]), finish([NT - 2]))
        in_turn(finish([NT - 1]))
        t_out = t_out[-1]
        sp.wait(t_out)
        three.close()

        block = top.enter_context(nc.Block())

        @block.sync
        def _(e):
            sp.run(e)

        @block.gpsimd
        def _(e):
            pool.run(e)

        @block.scalar
        def _(e):
            act.run(e)

        @block.vector
        def _(e):
            dve.run(e)

        @block.tensor
        def _(e):
            pe.run(e)


_INS = ['x', 'ctx_4096', 'L0_attn_freqs_cos', 'L0_attn_freqs_sin', 'L0_attn_wq', 'L0_attn_wk', 'L0_attn_wv',
        'L0_attn_wo', 'L0_attn_k_cache', 'L0_attn_v_cache', 'L0_attn_block_idx', 'L0_xattn_Wq', 'L0_xattn_bq',
        'L0_xattn_Wkv', 'L0_xattn_bkv', 'L0_xattn_Wo', 'L0_xattn_bo', 'L0_ffn_W', 'L0_ffn_b', 'L0_ffn_A',
        'L0_ffn_B', 'L0_ffn_p_scores']


def kernel(**inputs):
    import numpy as np
    import concourse.bacc as bacc
    from concourse.bass_utils import run_bass_kernel_spmd as run

    nc = bacc.Bacc("TRN2", target_bir_lowering=False, num_devices=1)
    arrays, args = {}, []
    for name in _INS:
        a = np.ascontiguousarray(inputs[name])
        arrays[f"in_{name}"] = a
        args.append(nc.dram_tensor(f"in_{name}", a.shape, mybir.dt.from_np(a.dtype), kind="ExternalInput").ap())
    o = nc.dram_tensor("out_0", (32, 64, 512), F32, kind="ExternalOutput").ap()
    decoder_kernel(nc, *args, o)
    r = run(nc, [arrays], core_ids=[0])
    return r.results[0]["out_0"]
```
